# Optimizing a Trainium2 kernel written in Bass

```python
import numpy as np
import jax
import jax.numpy as jnp

def _softmax(x, axis=-1):
    return jax.nn.softmax(x, axis=axis)

def _gelu(x):
    return jax.nn.gelu(x, approximate=True)

def _silu(x):
    return jax.nn.silu(x)

def _sigmoid(x):
    return jax.nn.sigmoid(x)

def _layernorm(x, axis=-1, eps=1e-05):
    m = jnp.mean(x, axis=axis, keepdims=True)
    v = jnp.var(x, axis=axis, keepdims=True)
    return (x - m) / jnp.sqrt(v + eps)

def _scatter_add(tgt, idx, src, axis=0):
    return tgt.at[idx].add(src)

def _segment_sum(src, seg, n):
    return jax.ops.segment_sum(src, seg, n)
kernel_name = 'mk_adaln_d1_jaxref_r8_c6724e'

def setup_inputs(seed: int=0):
    np.random.seed(seed)
    _w = jnp.asarray

    def _L0_attn_setup():
        import jax, jax.numpy as jnp
        import numpy as np
        Q_DIM = 512
        N_HEADS = 32
        HEAD_DIM = 128
        INNER = N_HEADS * HEAD_DIM
        EPS = 1e-06

        def rms_norm(x, w):
            xf = x.astype(jnp.float32)
            var = jnp.mean(xf * xf, axis=-1, keepdims=True)
            return (w.astype(jnp.float32) * xf * jax.lax.rsqrt(var + EPS)).astype(x.dtype)
        key = jax.random.key(seed)
        ks = jax.random.split(key, 12)
        s = 1.0 / np.sqrt(Q_DIM)
        return {'hidden_states': jax.random.normal(ks[0], (2, 256, Q_DIM), dtype=jnp.float32), 'Wq': jax.random.normal(ks[1], (Q_DIM, INNER), dtype=jnp.float32) * s, 'bq': jnp.zeros((INNER,), dtype=jnp.float32), 'Wk': jax.random.normal(ks[2], (Q_DIM, INNER), dtype=jnp.float32) * s, 'bk': jnp.zeros((INNER,), dtype=jnp.float32), 'Wv': jax.random.normal(ks[3], (Q_DIM, INNER), dtype=jnp.float32) * s, 'bv': jnp.zeros((INNER,), dtype=jnp.float32), 'Wo': jax.random.normal(ks[4], (INNER, Q_DIM), dtype=jnp.float32) * s, 'bo': jnp.zeros((Q_DIM,), dtype=jnp.float32), 'gq': jnp.ones((INNER,), dtype=jnp.float32), 'gk': jnp.ones((INNER,), dtype=jnp.float32)}
    _L0_attn_in = _L0_attn_setup()

    def _L0_ffn_setup():
        import jax, jax.numpy as jnp
        import numpy as np
        B_, S, D_IN, D_OUT = (4, 256, 512, 512)
        N, RANK, ALPHA = (8, 16, 32)
        SCALE = ALPHA / RANK
        key = jax.random.key(seed)
        kx, ka, kb, kw, kbias = jax.random.split(key, 5)
        x = jax.random.normal(kx, (B_, S, D_IN), dtype=jnp.float32)
        lora_A = jax.random.normal(ka, (N, RANK, D_IN), dtype=jnp.float32) * (1.0 / np.sqrt(D_IN))
        lora_B = jax.random.normal(kb, (N, D_OUT, RANK), dtype=jnp.float32) * (1.0 / np.sqrt(RANK))
        W = jax.random.normal(kw, (D_OUT, D_IN), dtype=jnp.float32) * (1.0 / np.sqrt(D_IN))
        bias = jax.random.normal(kbias, (D_OUT,), dtype=jnp.float32) * 0.01
        lora_weights = jnp.full((N,), 1.0 / N, dtype=jnp.float32)
        return {'x': x, 'lora_A': lora_A, 'lora_B': lora_B, 'W': W, 'bias': bias, 'lora_weights': lora_weights}
    _L0_ffn_in = _L0_ffn_setup()
    _L0_c = _w((lambda *s: np.random.randn(*s).astype(np.float32) * 0.05)(4, 512))
    _L0_wmod = _w((lambda *s: np.random.randn(*s).astype(np.float32) * 0.05)(512, 6 * 512) * 512 ** (-0.5))
    _d = {'L0_attn_hidden_states': _L0_attn_in['hidden_states'], 'L0_attn_Wq': _L0_attn_in['Wq'], 'L0_attn_bq': _L0_attn_in['bq'], 'L0_attn_Wk': _L0_attn_in['Wk'], 'L0_attn_bk': _L0_attn_in['bk'], 'L0_attn_Wv': _L0_attn_in['Wv'], 'L0_attn_bv': _L0_attn_in['bv'], 'L0_attn_Wo': _L0_attn_in['Wo'], 'L0_attn_bo': _L0_attn_in['bo'], 'L0_attn_gq': _L0_attn_in['gq'], 'L0_attn_gk': _L0_attn_in['gk'], 'L0_ffn_lora_A': _L0_ffn_in['lora_A'], 'L0_ffn_lora_B': _L0_ffn_in['lora_B'], 'L0_ffn_W': _L0_ffn_in['W'], 'L0_ffn_bias': _L0_ffn_in['bias'], 'L0_ffn_lora_weights': _L0_ffn_in['lora_weights'], 'L0_c': _L0_c, 'L0_wmod': _L0_wmod}
    _x0 = _d['L0_attn_hidden_states']
    _d['L0_attn_hidden_states'] = jax.random.normal(jax.random.fold_in(jax.random.key(seed), 1), (4, 256, 512), dtype=_x0.dtype)
    del _x0
    return _d

def reference(L0_attn_hidden_states, L0_attn_Wq, L0_attn_bq, L0_attn_Wk, L0_attn_bk, L0_attn_Wv, L0_attn_bv, L0_attn_Wo, L0_attn_bo, L0_attn_gq, L0_attn_gk, L0_ffn_lora_A, L0_ffn_lora_B, L0_ffn_W, L0_ffn_bias, L0_ffn_lora_weights, L0_c, L0_wmod):

    def _L0_attn_ref(hidden_states, Wq, bq, Wk, bk, Wv, bv, Wo, bo, gq, gk):
        import jax, jax.numpy as jnp
        import numpy as np
        Q_DIM = 512
        N_HEADS = 32
        HEAD_DIM = 128
        INNER = N_HEADS * HEAD_DIM
        EPS = 1e-06

        def rms_norm(x, w):
            xf = x.astype(jnp.float32)
            var = jnp.mean(xf * xf, axis=-1, keepdims=True)
            return (w.astype(jnp.float32) * xf * jax.lax.rsqrt(var + EPS)).astype(x.dtype)
        B, S, _ = hidden_states.shape
        q = hidden_states @ Wq + bq
        k = hidden_states @ Wk + bk
        v = hidden_states @ Wv + bv
        q = rms_norm(q, gq)
        k = rms_norm(k, gk)
        q = q.reshape(B, S, N_HEADS, HEAD_DIM).transpose(0, 2, 1, 3)
        k = k.reshape(B, S, N_HEADS, HEAD_DIM).transpose(0, 2, 1, 3)
        v = v.reshape(B, S, N_HEADS, HEAD_DIM).transpose(0, 2, 1, 3)
        scale = 1.0 / np.sqrt(HEAD_DIM)
        attn = jnp.einsum('bhqd,bhkd->bhqk', q.astype(jnp.float32), k.astype(jnp.float32)) * scale
        attn = jax.nn.softmax(attn, axis=-1)
        out = jnp.einsum('bhqk,bhkd->bhqd', attn, v.astype(jnp.float32))
        out = out.transpose(0, 2, 1, 3).reshape(B, S, INNER).astype(hidden_states.dtype)
        return out @ Wo + bo

    def _L0_ffn_ref(x, lora_A, lora_B, W, bias, lora_weights):
        import jax, jax.numpy as jnp
        import numpy as np
        B_, S, D_IN, D_OUT = (4, 256, 512, 512)
        N, RANK, ALPHA = (8, 16, 32)
        SCALE = ALPHA / RANK
        h = jnp.einsum('bsd,nrd->nbsr', x, lora_A)
        coef = (SCALE * lora_weights)[:, None, None]
        lora_out = jnp.einsum('nbsr,nor->bso', h, lora_B * coef)
        base = jnp.einsum('bsd,od->bso', x, W) + bias
        return base + lora_out
    x = L0_attn_hidden_states
    mod = (_silu(L0_c) @ L0_wmod).reshape(L0_c.shape[0], 6, 1, -1)
    sa, ca, ga, sb, cb, gb = (mod[:, 0], mod[:, 1], mod[:, 2], mod[:, 3], mod[:, 4], mod[:, 5])
    ga = (2 * (ga >= 0) - 1) * jnp.maximum(jnp.abs(ga), 0.25)
    gb = (2 * (gb >= 0) - 1) * jnp.maximum(jnp.abs(gb), 0.25)
    h = _layernorm(x, axis=-1) * (1 + ca) + sa
    x = x + ga * _L0_attn_ref(h, L0_attn_Wq, L0_attn_bq, L0_attn_Wk, L0_attn_bk, L0_attn_Wv, L0_attn_bv, L0_attn_Wo, L0_attn_bo, L0_attn_gq, L0_attn_gk)
    h = _layernorm(x, axis=-1) * (1 + cb) + sb
    x = x + gb * _L0_ffn_ref(h, L0_ffn_lora_A, L0_ffn_lora_B, L0_ffn_W, L0_ffn_bias, L0_ffn_lora_weights)
    return x

_drawn_inputs = setup_inputs


def setup_inputs(seed=0):
    import zlib

    import numpy as np

    out = dict(_drawn_inputs(seed))
    spreads = {'L0_attn_bq': (0.0, 0.8),
     'L0_attn_bk': (0.0, 0.8),
     'L0_attn_bv': (0.0, 0.1),
     'L0_attn_bo': (0.0, 0.338),
     'L0_attn_gq': (1.0, 0.6),
     'L0_attn_gk': (1.0, 0.6),
     'L0_ffn_lora_weights': (0.125, 0.2)}
    factors = {'L0_ffn_bias': 24.828}
    for name, (base, spread) in spreads.items():
        noise = np.random.default_rng([zlib.crc32(name.encode()), seed]).standard_normal(out[name].shape)
        drawn = base * np.exp(spread * noise) if base else spread * noise
        out[name] = jnp.asarray(drawn.astype(out[name].dtype))
    for name, factor in factors.items():
        out[name] = (out[name] * factor).astype(out[name].dtype)
    return out
```

```python
import concourse.bass as bass
from concourse import mybir
from concourse.alu_op_type import AluOpType as ALU
from contextlib import ExitStack


F32 = mybir.dt.float32
F32R = mybir.dt.float32r
ACT = mybir.ActivationFunctionType
AX = mybir.AxisListType

B, S, D = 4, 256, 512
H, HD = 32, 128
INNER = H * HD
T = B * S
P = 128
KT = D // P
NT = T // P
QT = S // P
HALF = T // 2
NG = H // 2
UNITS = 2 * B
NU = NG * UNITS
LN_EPS, RMS_EPS = 1e-5, 1e-6
SOFTMAX_SCALE = HD ** -0.5
NR, RANK = 8, 16
LORA_SCALE = 2.0
PARTS = ((0, 0), (0, 1), (1, 0))
SA, CA, GA, SB, CB, GB = range(6)


def after(eng, sem, n):
    if isinstance(n, int) and n <= 0:
        return
    eng.wait_ge(sem, n)


def loop_peeled(eng, n, body):
    body(0)
    with eng.Fori(1, n - 1) as i:
        body(i)
    body(n - 1)


def adaln_block(nc, x, wq, bq, wk, bk, wv, bv, wo, bo, gq, gk, lora_a, lora_b, w_ffn, b_ffn,
                lora_w, c, wmod, out):
    ctx = ExitStack()
    with ctx:
        def sb(name, shape, dt=F32):
            return ctx.enter_context(nc.sbuf_tensor(name, shape, dt))

        def sem(name):
            return ctx.enter_context(nc.semaphore(name))

        qk_dram = nc.dram_tensor("qk_spill", [H, 2, P, T], F32, kind="Internal").ap()
        gate_dram = nc.dram_tensor("gate_rows", [2, B, D], F32, kind="Internal").ap()

        hT = [sb("hT_hi", [P, KT, T], F32R), sb("hT_lo", [P, KT, T], F32R)]
        attn = sb("attn", [P, NT, D])
        v = [sb("v_hi", [P, NT, 2 * HD], F32R), sb("v_lo", [P, NT, 2 * HD], F32R)]
        wv_raw = sb("wv_raw", [P, KT, 2 * HD])
        wvs = [sb("wv_hi", [P, KT, 2 * HD], F32R), sb("wv_lo", [P, KT, 2 * HD], F32R)]
        wo_raw = sb("wo_raw", [P, 2, D])
        wos = [sb("wo_hi", [P, 2, D], F32R), sb("wo_lo", [P, 2, D], F32R)]
        qk_raw = sb("qk_raw", [P, 2, 2, T])
        qks = [sb("qk_hi", [P, 2, 2, T], F32R), sb("qk_lo", [P, 2, 2, T], F32R)]
        prob = sb("prob", [P, 2, QT, S])
        pT = [sb("pT_hi", [P, 2, QT, S], F32R), sb("pT_lo", [P, 2, QT, S], F32R)]
        oT = [sb("oT_hi", [P, 2, T], F32R), sb("oT_lo", [P, 2, T], F32R)]
        rk = sb("rk", [P, T])
        wstage = sb("wstage", [P, 4096])
        ident = sb("ident", [P, P])
        ones = sb("ones", [P, P])
        vec_rows = sb("vec_rows", [H, 5, HD])
        vec = sb("vec", [P, 5, H])
        vec_now = sb("vec_now", [P, 2, 5])
        c_row = sb("c_row", [B, 3, D])
        cT = sb("cT", [P, KT, B])
        mod1 = sb("mod1", [P, 2, KT, B])
        mod2 = sb("mod2", [P, 2, KT, B])
        stats = sb("stats", [P, NT, 6])
        mv = sb("mv", [P, NT, 2])
        norm = sb("norm", [P, 4, NT])
        qcol = sb("qcol", [P, 4, NT])
        qscale = sb("qscale", [P, 2, NT])
        rowmax = sb("rowmax", [P, 2, QT])
        negmax = sb("negmax", [P, 2, QT])
        rowsum = sb("rowsum", [P, 2, QT])
        rowinv = sb("rowinv", [P, 2, QT])
        lora_coef = sb("lora_coef", [P, 2])
        gate_row = sb("gate_row", [B, 2, D])
        gate_sign = sb("gate_sign", [B, 2, D])

        w_raw = wstage[:, 0:2048].rearrange("p (j w k n) -> p j w k n", j=2, w=2, k=KT)
        ws = [t[:, :, :, 0:D].rearrange("p j w (k n) -> p j w k n", k=KT) for t in qks]
        square = attn[:, 0:4, :]
        sumsq = attn[:, 4:8, :]
        x_sb = qk_raw[:, :, :, :].rearrange("p j w t -> p (j w t)").rearrange("p (n d) -> p n d", n=NT)
        wmod_a = attn[:, :, :].rearrange("p n d -> p (n d)").rearrange("p (k m) -> p k m", k=KT)
        wmod_b = wstage[:, :].rearrange("p (k m) -> p k m", k=KT)
        h_tmp = prob[:, :, :, :].rearrange("p a q s -> p a (q s)")
        ffn_raw = qk_raw[:, 0, :, :].rearrange("p w t -> p (w t)").rearrange("p (o d) -> p o d", o=KT)
        lora_a_raw = qk_raw[:, 1, 0, 0:D]
        lora_b_raw = qk_raw[:, 1, 0, D:2 * D]
        ffnT = [t[:, 0, :, :].rearrange("p w t -> p (w t)").rearrange("p (k o) -> p k o", k=KT) for t in qks]
        aT = [t[:, :, :].rearrange("p k n -> p (k n)")[:, 0:D] for t in wvs]
        bT = [t[:, :, :].rearrange("p k n -> p (k n)")[:, D:2 * D] for t in wvs]
        gates = wstage[:, :].rearrange("p (g b d) -> p g b d", g=2, b=B)
        bias_bc = wo_raw[:, 0, :]
        h2_tmp = rk[:, :].rearrange("p (a n) -> p a n", a=2)
        hlT = [t[:, 0:4, :].rearrange("p n d -> p (n d)") for t in v]
        gb_bias = wv_raw[:, :, :].rearrange("p k n -> p (k n)").rearrange("p (a d) -> p a d", a=2)

        bank = [ctx.enter_context(nc.psum_tensor(f"bank{i}", [P, 512], F32)) for i in range(8)]
        s_bank = [bank[0], bank[1]]
        pT_bank = [bank[2], bank[3]]
        o_bank = [bank[4], bank[5]]
        aux_bank = [bank[6], bank[7]]

        x_in = [sem(f"x_in{i}") for i in range(NT // 2)]
        small_in, mod_in = sem("small_in"), sem("mod_in")
        ident_ready, ones_ready = sem("ident_ready"), sem("ones_ready")
        dve_step = sem("dve_step")
        stat_ready, root_ready = sem("stat_ready"), sem("root_ready")
        c_exp, c_ready, cT_mm, cT_ready = sem("c_exp"), sem("c_ready"), sem("cT_mm"), sem("cT_ready")
        vec_mm, vec_ready = sem("vec_mm"), sem("vec_ready")
        vec_now_a, vec_now_b = sem("vec_now_a"), sem("vec_now_b")
        mod_mm, mod_ready = sem("mod_mm"), sem("mod_ready")
        xn_ready, hT_mm, h_affine, hT_hi_ready, hT_lo_ready = (
            sem("xn_ready"), sem("hT_mm"), sem("h_affine"), sem("hT_hi_ready"), sem("hT_lo_ready"))
        w_in = [sem("w_in0"), sem("w_in1")]
        w_hi, w_lo = sem("w_hi"), sem("w_lo")
        proj_mm, squared, summed, scaled = sem("proj_mm"), sem("squared"), sem("summed"), sem("scaled")
        spilled = [sem("spilled0"), sem("spilled1")]
        rms_mm, rms_var, rms_root, rms_ready = sem("rms_mm"), sem("rms_var"), sem("rms_root"), sem("rms_ready")
        wv_in, wo_in, bo_in = sem("wv_in"), sem("wo_in"), sem("bo_in")
        wv_hi, wv_lo, wo_hi, wo_lo = sem("wv_hi_done"), sem("wv_lo_done"), sem("wo_hi_done"), sem("wo_lo_done")
        qk_in = [sem("qk_in0"), sem("qk_in1")]
        k_normed, qk_hi, qk_lo = sem("k_normed"), sem("qk_hi_done"), sem("qk_lo_done")
        score_mm, max_done, negmax_done, exp_done, inv_done, prob_ready = (
            sem("score_mm"), sem("max_done"), sem("negmax_done"), sem("exp_done"), sem("inv_done"), sem("prob_ready"))
        pT_mm, pT_hi, pT_lo = sem("pT_mm"), sem("pT_hi_done"), sem("pT_lo_done")
        o_mm, o_hi, o_lo = sem("o_mm"), sem("o_hi_done"), sem("o_lo_done")
        v_mm, v_hi, v_lo = sem("v_mm"), sem("v_hi_done"), sem("v_lo_done")
        wo_mm, attn_added = sem("wo_mm"), sem("attn_added")
        ffn_in, ffn_mm, ffn_hi, ffn_lo = sem("ffn_in"), sem("ffn_mm"), sem("ffn_hi"), sem("ffn_lo")
        gate_stored, gate_in, bias_in, x_again = sem("gate_stored"), sem("gate_in"), sem("bias_in"), sem("x_again")
        gate_ready, gate_w_in = sem("gate_ready"), sem("gate_w_in")
        var2, root2, xn2, h2_mm, h2_affine, h2_hi, h2_lo = (
            sem("var2"), sem("root2"), sem("xn2"), sem("h2_mm"), sem("h2_affine"), sem("h2_hi"), sem("h2_lo"))
        hl_mm, hl_hi, hl_lo = sem("hl_mm"), sem("hl_hi"), sem("hl_lo")
        bias_gated, x_biased, out_mm, out_gated, out_ready, stored = (
            sem("bias_gated"), sem("x_biased"), sem("out_mm"), sem("out_gated"), sem("out_ready"), sem("stored"))

        x_tiles = x.rearrange("b (q p) d -> p (b q) d", p=P)
        out_tiles = out.rearrange("b (q p) d -> p (b q) d", p=P)
        wmod_t = wmod.rearrange("(k p) m -> p k m", p=P)
        w_t = [w.rearrange("(k p) (h n) -> h p k n", p=P, n=HD) for w in (wq, wk)]
        wv_t = wv.rearrange("(k p) (g n) -> g p k n", p=P, n=2 * HD)
        wo_t = wo.rearrange("(g j p) n -> g p j n", p=P, j=2)

        def at(ap, i):
            if isinstance(i, int):
                return ap[i]
            return ap[bass.ds(i, 1)].rearrange("o ... -> (o ...)") if len(ap.shape) == 1 else drop(ap[bass.ds(i, 1)])

        def drop(ap):
            names = "abcdefg"[:len(ap.shape) - 1]
            return ap.rearrange(f"o {' '.join(names)} -> (o {names[0]}) {' '.join(names[1:])}")

        block = ctx.enter_context(nc.Block())

        @block.sync
        def _(sp):
            for t in range(0, NT, 2):
                sp.dma_start(x_sb[:, t:t + 2, :], x_tiles[:, t:t + 2, :]).then_inc(x_in[t // 2], 16)

            def load_w(h, j):
                for w in range(2):
                    sp.dma_start(w_raw[:, j, w], at(w_t[w], h)).then_inc(w_in[j], 16)

            for j in range(2):
                load_w(j, j)

            def pair_a(g):
                for j in range(2):
                    h = 2 * g + j
                    if not (isinstance(g, int) and g == NG - 1):
                        after(sp, w_lo, 2 * h + 2)
                        load_w(h + 2, j)
                    for w in range(2):
                        after(sp, scaled, 4 * h + 2 * w + 2)
                        sp.dma_start(at(qk_dram, h)[w], qk_raw[:, j, w, :]).then_inc(spilled[j], 16)

            loop_peeled(sp, NG, pair_a)

            after(sp, w_lo, 2 * H)
            sp.dma_start(wmod_b[:, :, :], wmod_t[:, :, SB * D:(CB + 1) * D]).then_inc(mod_in, 16)

            def load_qk(g, j):
                for w in range(2):
                    sp.dma_start(qk_raw[:, j, w, :], at(qk_dram, 2 * g + j)[w]).then_inc(qk_in[j], 16)

            for j in range(2):
                after(sp, spilled[j], 32 * NG)
            for j in range(2):
                load_qk(0, j)
            after(sp, rms_ready, 2)
            sp.dma_start(attn[:, :, :], bo.rearrange("(a b d) -> a b d", a=1, b=1).to_broadcast([P, NT, D])).then_inc(bo_in, 16)

            def pair_b(g):
                last = isinstance(g, int) and g == NG - 1
                if not last:
                    for j in range(2):
                        after(sp, qk_lo, 2 * (2 * g + j) + 2)
                        load_qk(g + 1, j)

            loop_peeled(sp, NG, pair_b)

            after(sp, qk_lo, 2 * (H - 1))
            sp.dma_start(ffn_raw, w_ffn.rearrange("(o p) d -> p o d", p=P)).then_inc(ffn_in, 16)
            after(sp, qk_lo, 2 * H)
            sp.dma_start(lora_a_raw, lora_a.rearrange("n r d -> (n r) d")).then_inc(ffn_in, 16)
            for n in range(NR):
                sp.dma_start(lora_b_raw.rearrange("p (o n r) -> p o n r", n=NR, r=RANK)[:, :, n, :],
                             lora_b[n].rearrange("(o p) r -> p o r", p=P)).then_inc(ffn_in, 16)
            after(sp, wo_lo, NG)
            sp.dma_start(bias_bc, b_ffn.rearrange("(a d) -> a d", a=1).to_broadcast([P, D])).then_inc(bias_in, 16)
            after(sp, ffn_mm, 6)
            for t in range(0, NT, 2):
                sp.dma_start(x_sb[:, t:t + 2, :], x_tiles[:, t:t + 2, :]).then_inc(x_again, 16)
            after(sp, gate_ready, 2)
            sp.dma_start(gate_dram.rearrange("g b d -> b g d"), gate_row[:, :, :]).then_inc(gate_stored, 16)
            sp.wait_ge(gate_stored, 16)
            for g in range(2):
                sp.dma_start(gates[:, g], gate_dram[g].rearrange("(a b) d -> a b d", a=1).to_broadcast([P, B, D])).then_inc(gate_in, 16)
            for t in range(NT):
                after(sp, out_ready, t + 1)
                sp.dma_start(out_tiles[:, t, :], attn[:, t, :]).then_inc(stored, 16)
            sp.wait_ge(stored, 16 * NT)

        @block.gpsimd
        def _(pool):
            nc.gpsimd.memset(ones[:], 1.0).then_inc(ones_ready, 1)
            nc.gpsimd.memset(ident[:], 0.0).then_inc(ident_ready, 1)
            pool.wait_ge(ident_ready, 1)
            nc.gpsimd.affine_select(out=ident[:], in_=ident[:], compare_op=ALU.not_equal, fill=1.0, base=0,
                                    pattern=[[-1, P]], channel_multiplier=1).then_inc(ident_ready, 1)
            pool.dma_start(wv_raw[:, :, :], wv_t[0]).then_inc(wv_in, 16)
            pool.dma_start(wo_raw[:, :, :], wo_t[0]).then_inc(wo_in, 16)

            def pair_a(g):
                for j in range(2):
                    h = 2 * g + j
                    for s in range(4):
                        after(pool, squared, 4 * h + s + 1)
                        after(pool, summed, 4 * h - 4 + s + 1)
                        if isinstance(g, int) and h == 0:
                            nc.gpsimd.tensor_copy(sumsq[:, s], square[:, s]).then_inc(summed, 1)
                        else:
                            nc.gpsimd.tensor_tensor(sumsq[:, s], sumsq[:, s], square[:, s], ALU.add).then_inc(summed, 1)

            def split_lo(dst, raw, hi, done):
                nc.gpsimd.tensor_tensor(dst, raw, hi.bitcast(F32), ALU.subtract).then_inc(done, 1)

            def norm_k(g, j):
                after(pool, qk_in[j], 32 * (g + 1))
                nc.gpsimd.tensor_tensor(qk_raw[:, j, 1, :], qk_raw[:, j, 1, :], rk[:, :], ALU.mult).then_inc(k_normed, 1)

            def lo_qk(g, j):
                for w in range(2):
                    after(pool, qk_hi, 2 * (2 * g + j) + w + 1)
                    split_lo(qks[1][:, j, w, :], qk_raw[:, j, w, :], qks[0][:, j, w, :], qk_lo)

            def lo_wv(g):
                after(pool, wv_hi, g + 1)
                split_lo(wvs[1][:, :, :], wv_raw[:, :, :], wvs[0][:, :, :], wv_lo)

            def lo_wo(g):
                after(pool, wo_hi, g + 1)
                split_lo(wos[1][:, :, :], wo_raw[:, :, :], wos[0][:, :, :], wo_lo)

            lo_wv(0)
            loop_peeled(pool, NG, pair_a)
            pool.wait_ge(rms_ready, 1)
            for j in range(2):
                norm_k(0, j)
                lo_qk(0, j)

            def pair_b(g):
                last = isinstance(g, int) and g == NG - 1
                if not last:
                    after(pool, wv_lo, g + 1)
                    pool.dma_start(wv_raw[:, :, :], at(wv_t, g + 1)).then_inc(wv_in, 16)
                    norm_k(g + 1, 0)
                    lo_wv(g + 1)
                    lo_qk(g + 1, 0)
                lo_wo(g)
                if not last:
                    after(pool, wo_lo, g + 1)
                    pool.dma_start(wo_raw[:, :, :], at(wo_t, g + 1)).then_inc(wo_in, 16)
                    norm_k(g + 1, 1)
                    lo_qk(g + 1, 1)
                else:
                    after(pool, mod_ready, 4)
                    for i, m in enumerate((GA, GB)):
                        pool.dma_start(wmod_b[:, :, i * D:(i + 1) * D], wmod_t[:, :, m * D:(m + 1) * D]).then_inc(gate_w_in, 16)

            loop_peeled(pool, NG, pair_b)

            pool.wait_ge(gate_in, 32)
            pool.wait_ge(bias_in, 16)
            for b in range(B):
                after(pool, x_biased, 2 * b - 2)
                nc.gpsimd.tensor_tensor(gb_bias[:, b % 2], gates[:, 1, b], bias_bc, ALU.mult).then_inc(bias_gated, 1)
                pool.wait_ge(bias_gated, b + 1)
                for t in (2 * b, 2 * b + 1):
                    pool.wait_ge(xn2, t + 1)
                    nc.gpsimd.tensor_tensor(x_sb[:, t], x_sb[:, t], gb_bias[:, b % 2], ALU.add).then_inc(x_biased, 1)

        @block.scalar
        def _(act):
            act.dma_start(c_row[:, 0, :], c).then_inc(small_in, 16)
            for i, a in enumerate((bq, bk, gq, gk, bv)):
                act.dma_start(vec_rows[:, i, :], a.rearrange("(h n) -> h n", n=HD)).then_inc(small_in, 16)
            act.dma_start(wmod_a[:, :, :], wmod_t[:, :, 0:2 * D]).then_inc(mod_in, 16)
            lw = lora_w.rearrange("(n a b) -> n a b", a=1, b=1)
            act.dma_start(lora_coef[:, 0:1], lw.to_broadcast([NR, RANK, 1])).then_inc(small_in, 16)

            act.wait_ge(small_in, 112)
            nc.scalar.activation(c_row[:, 1, :], c_row[:, 0, :], ACT.Exp, scale=-1.0).then_inc(c_exp, 1)
            act.wait_ge(stat_ready, 1)
            nc.scalar.activation(norm[:, 1, :], norm[:, 0, :], ACT.Sqrt).then_inc(root_ready, 1)

            for n in range(2 * KT):
                half, k = divmod(n, KT)
                act.wait_ge(hT_mm, n + 1)
                if n == 0:
                    act.wait_ge(mod_ready, 2)
                if n >= 2:
                    act.wait_ge(hT_lo_ready, n - 1)
                for i in range(2):
                    b = 2 * half + i
                    nc.scalar.activation(h_tmp[:, n % 2, i * S:(i + 1) * S], bank[n][:, i * S:(i + 1) * S], ACT.Identity,
                                         scale=mod1[:, 1, k, b:b + 1], bias=mod1[:, 0, k, b:b + 1]).then_inc(h_affine, 1)

            def pair_a(g):
                for j in range(2):
                    h = 2 * g + j
                    for s in range(4):
                        w = s // 2
                        after(act, proj_mm, 4 * h + s + 1)
                        after(act, summed, 4 * h - 4 + s + 1)
                        if s == 0:
                            after(act, vec_now_a, h + 1)
                        nc.scalar.activation(square[:, s], bank[4 * j + s][:, :], ACT.Square,
                                             bias=vec_now[:, j, w:w + 1]).then_inc(squared, 1)

            def hi_copy(dst, src, done):
                nc.scalar.activation(dst, src, ACT.Copy).then_inc(done, 1)

            def hi_wv(g):
                after(act, wv_in, 16 * (g + 1))
                after(act, v_mm, 8 * g)
                hi_copy(wvs[0][:, :, :], wv_raw[:, :, :], wv_hi)

            def hi_wo(g):
                after(act, wo_in, 16 * (g + 1))
                after(act, wo_mm, 8 * g)
                hi_copy(wos[0][:, :, :], wo_raw[:, :, :], wo_hi)

            def hi_qk(g, j, w):
                h = 2 * g + j
                if w:
                    after(act, k_normed, h + 1)
                else:
                    after(act, qk_in[j], 32 * (g + 1))
                after(act, score_mm, 4 * (h - 1))
                if isinstance(g, int) and g == 0:
                    act.wait_ge(proj_mm, 4 * H)
                hi_copy(qks[0][:, j, w, :], qk_raw[:, j, w, :], qk_hi)

            def hi_v(n, s):
                after(act, v_mm, n + 1)
                hi_copy(v[0][:, s, :], aux_bank[s % 2][:, 0:2 * HD], v_hi)

            def exp(g, u, i):
                b = i % B
                after(act, negmax_done, u + 1)
                after(act, pT_mm, u - 1)
                for q in range(QT):
                    t = QT * b + q
                    nc.scalar.activation(prob[:, i % 2, q, :], s_bank[i % 2][:, q * S:(q + 1) * S], ACT.Exp,
                                         scale=qscale[:, 0, t:t + 1], bias=negmax[:, i % 2, q:q + 1],
                                         accum_out=rowsum[:, i % 2, q:q + 1]).then_inc(exp_done, 1)

            def hi_pT(u, i):
                after(act, pT_mm, u + 1)
                after(act, o_mm, u - 1)
                hi_copy(pT[0][:, i % 2, :, :], pT_bank[i % 2][:, :].rearrange("p (k q) -> p k q", k=QT), pT_hi)

            def hi_o(u, i, h):
                j, b = divmod(i, B)
                after(act, o_mm, u + 1)
                if b == 0:
                    after(act, vec_now_b, h + 1)
                nc.scalar.activation(oT[0][:, j, b * S:(b + 1) * S], o_bank[i % 2][:, 0:S], ACT.Identity,
                                     bias=vec_now[:, j, 4:5]).then_inc(o_hi, 1)

            hi_wv(0)
            loop_peeled(act, NG, pair_a)

            for s in range(2):
                hi_v(s, s)
            act.wait_ge(rms_var, 1)
            nc.scalar.activation(qcol[:, 1, :], qcol[:, 0, :], ACT.Sqrt).then_inc(rms_root, 1)
            act.wait_ge(rms_var, 3)
            nc.scalar.activation(attn[:, 0:2, :].rearrange("p a n -> p (a n)"), rk[:, :], ACT.Sqrt).then_inc(rms_root, 1)
            hi_qk(0, 0, 0)
            for s in range(2, NT):
                hi_v(s, s)
            hi_qk(0, 0, 1)
            hi_qk(0, 1, 0)
            hi_qk(0, 1, 1)
            exp(0, 0, 0)
            exp(0, 1, 1)
            hi_pT(0, 0)

            def pair_b(g):
                first, last = isinstance(g, int) and g == 0, isinstance(g, int) and g == NG - 1
                for i in range(UNITS):
                    u = UNITS * g + i
                    if not (last and i + 2 >= UNITS):
                        exp(g, u + 2, (i + 2) % UNITS)
                    if not (last and i + 1 >= UNITS):
                        hi_pT(u + 1, (i + 1) % UNITS)
                    if i == 0 and not last:
                        hi_wv(g + 1)
                    if i in (1, 2) and not last:
                        hi_qk(g + 1, 0, i - 1)
                    if i == 4:
                        hi_wo(g)
                    if i in (5, 6) and not last:
                        hi_qk(g + 1, 1, i - 5)
                    hi_o(u, i, 2 * g + i // B)
                    if i >= B and not last:
                        for t in range(2):
                            s = 2 * (i - B) + t
                            hi_v(8 * (g + 1) + s, s)
                    if i >= B and last:
                        for n in (2 * (i - B), 2 * (i - B) + 1):
                            hi_ffn(n)

            def hi_ffn(n):
                if n >= 6:
                    return
                act.wait_ge(ffn_mm, n + 1)
                ps = aux_bank[n % 2]
                if n < 4:
                    hi_copy(ffnT[0][:, n, :], ps[:, :], ffn_hi)
                elif n == 4:
                    hi_copy(aT[0], ps[:, :], ffn_hi)
                else:
                    act.wait_ge(dve_step, 1)
                    nc.scalar.activation(bT[0], ps[:, :], ACT.Copy, scale=lora_coef[:, 1:2]).then_inc(ffn_hi, 1)

            loop_peeled(act, NG, pair_b)

            def root(b):
                act.wait_ge(var2, b + 1)
                nc.scalar.activation(norm[:, 1, 2 * b:2 * b + 2], norm[:, 0, 2 * b:2 * b + 2], ACT.Sqrt).then_inc(root2, 1)

            def affine(b):
                for half in range(2):
                    n = 2 * b + half
                    act.wait_ge(h2_mm, n + 1)
                    after(act, h2_lo, n - 1)
                    for i in range(2):
                        k = 2 * half + i
                        nc.scalar.activation(h2_tmp[:, n % 2, i * S:(i + 1) * S], bank[half][:, i * S:(i + 1) * S],
                                             ACT.Identity, scale=mod2[:, 1, k, b:b + 1],
                                             bias=mod2[:, 0, k, b:b + 1]).then_inc(h2_affine, 1)
                    act.wait_ge(h2_affine, 2 * n + 2)
                    nc.scalar.activation(hT[0][:, 2 * half:2 * half + 2, b * S:(b + 1) * S],
                                         h2_tmp[:, n % 2, :].rearrange("p (k t) -> p k t", k=2), ACT.Copy).then_inc(h2_hi, 1)

            def hi_hl(b):
                act.wait_ge(hl_mm, b + 1)
                hi_copy(hlT[0][:, b * S:(b + 1) * S], bank[2 + b % 2][:, 0:S], hl_hi)

            for b in range(B + 2):
                if b < B:
                    root(b)
                if 1 <= b <= B:
                    affine(b - 1)
                if b >= 2:
                    hi_hl(b - 2)

        @block.vector
        def _(dve):
            steps = [0]

            def link(ins):
                steps[0] += 1
                ins.then_inc(dve_step, 1)
                dve.wait_ge(dve_step, steps[0])

            def newton(y, var, tmp):
                link(nc.vector.tensor_tensor(tmp, y, y, ALU.mult))
                link(nc.vector.tensor_tensor(tmp, tmp, var, ALU.mult))
                link(nc.vector.tensor_scalar(tmp, tmp, -0.5, 1.5, ALU.mult, ALU.add))
                return nc.vector.tensor_tensor(y, y, tmp, ALU.mult)

            dve.wait_ge(small_in, 112)
            link(nc.vector.tensor_scalar(lora_coef[:, 1:2], lora_coef[:, 0:1], LORA_SCALE, None, ALU.mult))
            dve.wait_ge(c_exp, 1)
            link(nc.vector.tensor_scalar(c_row[:, 1, :], c_row[:, 1, :], 1.0, None, ALU.add))
            link(nc.vector.reciprocal(c_row[:, 2, :], c_row[:, 1, :]))
            nc.vector.tensor_tensor(c_row[:, 1, :], c_row[:, 0, :], c_row[:, 2, :], ALU.mult).then_inc(c_ready, 1)

            for t in range(NT):
                if t % 2 == 0:
                    dve.wait_ge(x_in[t // 2], 16)
                last = nc.vector.bn_stats(stats[:, t, :], x_sb[:, t, :])
            link(last)
            for t in range(NT):
                last = nc.vector.bn_aggr(mv[:, t, :], stats[:, t, :])
            link(last)
            link(nc.vector.tensor_scalar(norm[:, 0, :], mv[:, :, 1], LN_EPS, None, ALU.add))
            nc.vector.tensor_copy(norm[:, 3, :], mv[:, :, 0]).then_inc(stat_ready, 1)

            dve.wait_ge(cT_mm, 1)
            nc.vector.tensor_copy(cT[:, :, :], bank[0][:, 0:KT * B].rearrange("p (k b) -> p k b", k=KT)).then_inc(cT_ready, 1)

            dve.wait_ge(root_ready, 1)
            link(nc.vector.reciprocal(norm[:, 2, :], norm[:, 1, :]))
            link(newton(norm[:, 2, :], norm[:, 0, :], norm[:, 3, :]))
            for t in range(NT):
                nc.vector.tensor_scalar(x_sb[:, t, :], x_sb[:, t, :], mv[:, t, 0:1], norm[:, 2, t:t + 1],
                                        ALU.subtract, ALU.mult).then_inc(xn_ready, 1)

            def modulation(dst, ps, n):
                cols = ps[:, 0:2 * KT * B].rearrange("p (m k b) -> p m k b", m=2, k=KT)
                dve.wait_ge(mod_mm, n + 1)
                nc.vector.tensor_copy(dst[:, 0], cols[:, 0]).then_inc(mod_ready, 1)
                nc.vector.tensor_scalar(dst[:, 1], cols[:, 1], 1.0, None, ALU.add).then_inc(mod_ready, 1)

            modulation(mod1, bank[1], 0)
            dve.wait_ge(vec_mm, 1)
            nc.vector.tensor_copy(vec[:, :, :], bank[2][:, 0:5 * H].rearrange("p (a h) -> p a h", a=5)).then_inc(vec_ready, 1)

            for n in range(2 * KT):
                half, k = divmod(n, KT)
                dve.wait_ge(h_affine, 2 * n + 2)
                hi = hT[0][:, k, half * HALF:(half + 1) * HALF]
                nc.vector.tensor_copy(hi, h_tmp[:, n % 2, :]).then_inc(hT_hi_ready, 1)
                dve.wait_ge(hT_hi_ready, n + 1)
                nc.vector.tensor_tensor(hT[1][:, k, half * HALF:(half + 1) * HALF], h_tmp[:, n % 2, :], hi.bitcast(F32),
                                        ALU.subtract).then_inc(hT_lo_ready, 1)

            def split_w(g, j):
                h = 2 * g + j
                after(dve, w_in[j], 32 * (g + 1))
                after(dve, proj_mm, 4 * (h - 1))
                for w in range(2):
                    nc.vector.tensor_copy(ws[0][:, j, w], w_raw[:, j, w]).then_inc(w_hi, 1)
                for w in range(2):
                    after(dve, w_hi, 2 * h + w + 1)
                    nc.vector.tensor_tensor(ws[1][:, j, w], w_raw[:, j, w], ws[0][:, j, w].bitcast(F32),
                                            ALU.subtract).then_inc(w_lo, 1)

            def take_vectors(h, j, done):
                src = vec[:, :, h:h + 1] if isinstance(h, int) else vec[:, :, bass.ds(h, 1)]
                nc.vector.tensor_scalar(vec_now[:, j, :], src.rearrange("p a o -> p (a o)"), 1.0, None, ALU.mult).then_inc(done, 1)

            split_w(0, 0)
            dve.wait_ge(vec_ready, 1)

            def pair_a(g):
                for j in range(2):
                    h = 2 * g + j
                    if j == 0:
                        split_w(g, 1)
                    elif not (isinstance(g, int) and g == NG - 1):
                        split_w(g + 1, 0)
                    after(dve, squared, 4 * (h - 1))
                    take_vectors(h, j, vec_now_a)
                    after(dve, spilled[j], 32 * g)
                    after(dve, vec_now_a, h + 1)
                    for s in range(4):
                        w, half = divmod(s, 2)
                        after(dve, squared, 4 * h + s + 1)
                        nc.vector.tensor_scalar(qk_raw[:, j, w, half * HALF:(half + 1) * HALF], bank[4 * j + s][:, :],
                                                vec_now[:, j, w:w + 1], vec_now[:, j, 2 + w:3 + w],
                                                ALU.add, ALU.mult).then_inc(scaled, 1)

            loop_peeled(dve, NG, pair_a)

            def lo_v(n, s):
                after(dve, v_hi, n + 1)
                nc.vector.tensor_tensor(v[1][:, s, :], aux_bank[s % 2][:, 0:2 * HD], v[0][:, s, :].bitcast(F32),
                                        ALU.subtract).then_inc(v_lo, 1)

            for s in range(2):
                lo_v(s, s)
            dve.wait_ge(rms_mm, 1)
            nc.vector.tensor_scalar(qcol[:, 0, :], bank[2][:, 0:NT], 1.0 / INNER, RMS_EPS, ALU.mult, ALU.add).then_inc(rms_var, 1)
            dve.wait_ge(rms_mm, 3)
            for i in range(2):
                nc.vector.tensor_scalar(rk[:, i * HALF:(i + 1) * HALF], bank[i][:, :], 1.0 / INNER, RMS_EPS,
                                        ALU.mult, ALU.add).then_inc(rms_var, 1)
            ry = attn[:, 0:2, :].rearrange("p a n -> p (a n)")
            rt = attn[:, 2:4, :].rearrange("p a n -> p (a n)")
            dve.wait_ge(rms_root, 2)
            link(nc.vector.reciprocal(ry, ry))
            link(nc.vector.tensor_tensor(rt, ry, ry, ALU.mult))
            link(nc.vector.tensor_tensor(rt, rt, rk[:, :], ALU.mult))
            link(nc.vector.tensor_scalar(rt, rt, -0.5, 1.5, ALU.mult, ALU.add))
            nc.vector.tensor_tensor(rk[:, :], ry, rt, ALU.mult).then_inc(rms_ready, 1)
            link(nc.vector.reciprocal(qcol[:, 2, :], qcol[:, 1, :]))
            link(newton(qcol[:, 2, :], qcol[:, 0, :], qcol[:, 3, :]))
            nc.vector.tensor_scalar(qscale[:, 0, :], qcol[:, 2, :], SOFTMAX_SCALE, None, ALU.mult)
            nc.vector.tensor_scalar(qscale[:, 1, :], qcol[:, 2, :], -SOFTMAX_SCALE, None, ALU.mult).then_inc(rms_ready, 1)
            for s in range(2, NT):
                lo_v(s, s)
            modulation(mod2, bank[3], 1)

            def maxima(u, i):
                b = i % B
                after(dve, score_mm, u + 1)
                nc.vector.tensor_reduce(rowmax[:, i % 2, :], s_bank[i % 2][:, :].rearrange("p (q s) -> p q s", q=QT),
                                        AX.X, ALU.max).then_inc(max_done, 1)
                after(dve, max_done, u + 1)
                nc.vector.tensor_tensor(negmax[:, i % 2, :], rowmax[:, i % 2, :], qscale[:, 1, QT * b:QT * (b + 1)],
                                        ALU.mult).then_inc(negmax_done, 1)

            def normalise(u, i):
                after(dve, exp_done, QT * (u + 1))
                nc.vector.reciprocal(rowinv[:, i % 2, :], rowsum[:, i % 2, :]).then_inc(inv_done, 1)
                after(dve, inv_done, u + 1)
                for q in range(QT):
                    last = nc.vector.tensor_scalar(prob[:, i % 2, q, :], prob[:, i % 2, q, :], rowinv[:, i % 2, q:q + 1],
                                                   None, ALU.mult)
                last.then_inc(prob_ready, 1)

            def lo_pT(u, i):
                after(dve, pT_hi, u + 1)
                nc.vector.tensor_tensor(pT[1][:, i % 2, :, :], pT_bank[i % 2][:, :].rearrange("p (k q) -> p k q", k=QT),
                                        pT[0][:, i % 2, :, :].bitcast(F32), ALU.subtract).then_inc(pT_lo, 1)

            def lo_o(u, i, h):
                j, b = divmod(i, B)
                after(dve, o_hi, u + 1)
                after(dve, vec_now_b, h + 1)
                nc.vector.scalar_tensor_tensor(out=oT[1][:, j, b * S:(b + 1) * S], in0=o_bank[i % 2][:, 0:S],
                                               scalar=vec_now[:, j, 4:5], in1=oT[0][:, j, b * S:(b + 1) * S].bitcast(F32),
                                               op0=ALU.add, op1=ALU.subtract).then_inc(o_lo, 1)

            def add_attn(g, t):
                after(dve, wo_mm, 8 * g + t + 1)
                nc.vector.tensor_tensor(attn[:, t, :], aux_bank[t % 2][:, :], attn[:, t, :], ALU.add).then_inc(attn_added, 1)

            maxima(0, 0)
            maxima(1, 1)
            normalise(0, 0)
            lo_pT(0, 0)
            maxima(2, 2)
            normalise(1, 1)
            dve.wait_ge(bo_in, 16)

            def pair_b(g):
                first, last = isinstance(g, int) and g == 0, isinstance(g, int) and g == NG - 1
                for i in range(UNITS):
                    u = UNITS * g + i
                    if not (last and i + 1 >= UNITS):
                        lo_pT(u + 1, (i + 1) % UNITS)
                    if not (last and i + 3 >= UNITS):
                        maxima(u + 3, (i + 3) % UNITS)
                    if not (last and i + 2 >= UNITS):
                        normalise(u + 2, (i + 2) % UNITS)
                    if i < B and not first:
                        for t in (2 * i, 2 * i + 1):
                            add_attn(g - 1, t)
                    if i % B == 0:
                        after(dve, o_hi, UNITS * (g - 1) + i + B)
                        take_vectors(2 * g + i // B, i // B, vec_now_b)
                    lo_o(u, i, 2 * g + i // B)
                    if i >= B and not last:
                        for s in (2 * (i - B), 2 * (i - B) + 1):
                            lo_v(8 * (g + 1) + s, s)
                    if i >= B and last:
                        for n in (2 * (i - B), 2 * (i - B) + 1):
                            lo_ffn(n)

            def lo_ffn(n):
                ps = aux_bank[n % 2]
                if n < 6:
                    dve.wait_ge(ffn_hi, n + 1)
                if n < 4:
                    nc.vector.tensor_tensor(ffnT[1][:, n, :], ps[:, :], ffnT[0][:, n, :].bitcast(F32), ALU.subtract).then_inc(ffn_lo, 1)
                elif n == 4:
                    nc.vector.tensor_tensor(aT[1], ps[:, :], aT[0].bitcast(F32), ALU.subtract).then_inc(ffn_lo, 1)
                elif n == 5:
                    nc.vector.scalar_tensor_tensor(out=bT[1], in0=ps[:, :], scalar=lora_coef[:, 1:2], in1=bT[0].bitcast(F32),
                                                   op0=ALU.mult, op1=ALU.subtract).then_inc(ffn_lo, 1)
                else:
                    m = n - 6
                    dve.wait_ge(ffn_mm, n + 1)
                    link(nc.vector.tensor_copy(gate_row[:, m, :], ps[0:B, :]))
                    link(nc.vector.tensor_scalar(gate_sign[:, m, :], gate_row[:, m, :], 0.0, 2.0, ALU.is_ge, ALU.mult))
                    link(nc.vector.tensor_scalar(gate_sign[:, m, :], gate_sign[:, m, :], 1.0, None, ALU.subtract))
                    link(nc.vector.tensor_tensor(gate_row[:, m, :], gate_row[:, m, :], gate_sign[:, m, :], ALU.mult))
                    nc.vector.scalar_tensor_tensor(out=gate_row[:, m, :], in0=gate_row[:, m, :], scalar=0.25,
                                                   in1=gate_sign[:, m, :], op0=ALU.max, op1=ALU.mult).then_inc(gate_ready, 1)

            loop_peeled(dve, NG, pair_b)

            def residual(b):
                for t in (2 * b, 2 * b + 1):
                    add_attn(NG - 1, t)
                    dve.wait_ge(attn_added, 8 * (NG - 1) + t + 1)
                    link(nc.vector.tensor_tensor(attn[:, t, :], attn[:, t, :], gates[:, 0, b, :], ALU.mult))
                    link(nc.vector.tensor_tensor(x_sb[:, t, :], attn[:, t, :], x_sb[:, t, :], ALU.add))
                    link(nc.vector.bn_stats(stats[:, t, :], x_sb[:, t, :]))
                    link(nc.vector.bn_aggr(mv[:, t, :], stats[:, t, :]))
                nc.vector.tensor_scalar(norm[:, 0, 2 * b:2 * b + 2], mv[:, 2 * b:2 * b + 2, 1], LN_EPS, None, ALU.add).then_inc(var2, 1)

            def normed(b):
                two = slice(2 * b, 2 * b + 2)
                dve.wait_ge(root2, b + 1)
                link(nc.vector.reciprocal(norm[:, 2, two], norm[:, 1, two]))
                link(newton(norm[:, 2, two], norm[:, 0, two], norm[:, 3, two]))
                for t in (2 * b, 2 * b + 1):
                    nc.vector.tensor_scalar(attn[:, t, :], x_sb[:, t, :], mv[:, t, 0:1], norm[:, 2, t:t + 1],
                                            ALU.subtract, ALU.mult).then_inc(xn2, 1)

            def lo_h2(b):
                for half in range(2):
                    n = 2 * b + half
                    dve.wait_ge(h2_hi, n + 1)
                    part = (slice(None), slice(2 * half, 2 * half + 2), slice(b * S, (b + 1) * S))
                    nc.vector.tensor_tensor(hT[1][part], h2_tmp[:, n % 2, :].rearrange("p (k t) -> p k t", k=2),
                                            hT[0][part].bitcast(F32), ALU.subtract).then_inc(h2_lo, 1)

            def lo_hl(b):
                dve.wait_ge(hl_hi, b + 1)
                nc.vector.tensor_tensor(hlT[1][:, b * S:(b + 1) * S], bank[2 + b % 2][:, 0:S],
                                        hlT[0][:, b * S:(b + 1) * S].bitcast(F32), ALU.subtract).then_inc(hl_lo, 1)

            def finish(b):
                for t in (2 * b, 2 * b + 1):
                    dve.wait_ge(out_mm, t + 1)
                    nc.vector.tensor_tensor(attn[:, t, :], bank[4 + t % 2][:, :], gates[:, 1, b, :], ALU.mult).then_inc(out_gated, 1)
                    dve.wait_ge(out_gated, t + 1)
                    dve.wait_ge(x_biased, t + 1)
                    nc.vector.tensor_tensor(attn[:, t, :], attn[:, t, :], x_sb[:, t, :], ALU.add).then_inc(out_ready, 1)

            dve.wait_ge(gate_in, 32)
            dve.wait_ge(x_again, 16 * (NT // 2))
            for b in range(B + 3):
                if b < B:
                    residual(b)
                if b >= 1 and b - 1 < B:
                    lo_h2(b - 1)
                if b < B:
                    normed(b)
                if b >= 2 and b - 2 < B:
                    lo_hl(b - 2)
                if b >= 3:
                    finish(b - 3)

        @block.tensor
        def _(pe):
            mm = nc.tensor.matmul

            def product(out_, lhs, rhs, steps):
                n = len(steps) * len(PARTS)
                for i, (k, (a, b)) in enumerate([(k, p) for k in steps for p in PARTS]):
                    last = mm(out_, lhs(a, k), rhs(b, k), start=i == 0, stop=i == n - 1)
                return last

            pe.wait_ge(ident_ready, 2)
            pe.wait_ge(c_ready, 1)
            for k in range(KT):
                last = nc.tensor.transpose(bank[0][:, k * B:(k + 1) * B], c_row[:, 1, k * P:(k + 1) * P], ident[0:B, 0:B])
            last.then_inc(cT_mm, 1)
            for i in range(5):
                last = nc.tensor.transpose(bank[2][:, i * H:(i + 1) * H], vec_rows[:, i, :], ident[0:H, 0:H])
            last.then_inc(vec_mm, 1)

            def mod_columns(ps, w):
                for m in range(2 * KT):
                    for k in range(KT):
                        last = mm(ps[:, m * B:(m + 1) * B], w[:, k, m * P:(m + 1) * P], cT[:, k, :],
                                  start=k == 0, stop=k == KT - 1)
                return last

            pe.wait_ge(cT_ready, 1)
            pe.wait_ge(mod_in, 16)
            mod_columns(bank[1], wmod_a).then_inc(mod_mm, 1)

            for n in range(2 * KT):
                half, k = divmod(n, KT)
                pe.wait_ge(xn_ready, 4 * half + 4)
                if n == 1:
                    pe.wait_ge(mod_ready, 2)
                if n == 2:
                    pe.wait_ge(vec_ready, 1)
                for t in range(4):
                    last = nc.tensor.transpose(bank[n][:, t * P:(t + 1) * P], x_sb[:, 4 * half + t, k * P:(k + 1) * P], ident[:])
                last.then_inc(hT_mm, 1)

            pe.wait_ge(hT_lo_ready, 2 * KT)

            def pair_a(g):
                for j in range(2):
                    h = 2 * g + j
                    for w in range(2):
                        after(pe, w_lo, 2 * h + w + 1)
                        after(pe, scaled, 4 * (h - 2) + 2 * w + 2)
                        for k in range(KT):
                            for i, (a, b) in enumerate(PARTS):
                                for half in range(2):
                                    done = k == KT - 1 and i == len(PARTS) - 1
                                    last = mm(bank[4 * j + 2 * w + half][:, :], ws[a][:, j, w, k, :],
                                              hT[b][:, k, half * HALF:(half + 1) * HALF],
                                              start=k == 0 and i == 0, stop=done)
                                    if done:
                                        last.then_inc(proj_mm, 1)

            loop_peeled(pe, NG, pair_a)

            def values(g, s):
                n = 8 * g + s
                after(pe, wv_lo, g + 1)
                if s < 2 and isinstance(g, int) and g == 0:
                    pe.wait_ge(scaled, 4 * H)
                elif s >= 2 or (isinstance(g, int) and g == 1):
                    after(pe, v_lo, n - 1)
                else:
                    after(pe, attn_added, 8 * (g - 2) + 6 + s + 1)
                product(aux_bank[s % 2][:, 0:2 * HD], lambda a, k: hT[a][:, k, s * P:(s + 1) * P],
                        lambda b, k: wvs[b][:, k, :], range(KT)).then_inc(v_mm, 1)

            for s in range(2):
                values(0, s)
            pe.wait_ge(summed, 4 * H)
            for t in range(NT):
                last = mm(bank[2][:, t:t + 1], sumsq[:, t // 4, (t % 4) * P:(t % 4 + 1) * P], ones[:, 0:1], start=True, stop=True)
            last.then_inc(rms_mm, 1)
            for i in range(2):
                mm(bank[i][:, :], ones[:], sumsq[:, 2 + i, :], start=True, stop=True).then_inc(rms_mm, 1)
            for s in range(2, NT):
                values(0, s)
            pe.wait_ge(mod_in, 32)
            mod_columns(bank[3], wmod_b).then_inc(mod_mm, 1)

            def scores(g, u, i):
                j, b = divmod(i, B)
                if b == 0:
                    after(pe, qk_lo, 2 * (2 * g + j) + 2)
                for q in range(QT):
                    rows = slice(b * S + q * P, b * S + (q + 1) * P)
                    last = product(s_bank[i % 2][:, q * S:(q + 1) * S], lambda a, _: qks[a][:, j, 0, rows],
                                   lambda a, _: qks[a][:, j, 1, b * S:(b + 1) * S], [0])
                last.then_inc(score_mm, 1)

            def transposes(u, i):
                after(pe, prob_ready, u + 1)
                after(pe, pT_lo, u - 1)
                for k in range(QT):
                    for q in range(QT):
                        last = nc.tensor.transpose(pT_bank[i % 2][:, k * S + q * P:k * S + (q + 1) * P],
                                                   prob[:, i % 2, q, k * P:(k + 1) * P], ident[:])
                last.then_inc(pT_mm, 1)

            def weigh(g, u, i):
                j, b = divmod(i, B)
                after(pe, pT_lo, u + 1)
                after(pe, v_lo, 8 * g + 2 * b + 2)
                after(pe, o_lo, u - 1)
                product(o_bank[i % 2][:, 0:S], lambda a, k: v[a][:, 2 * b + k, j * HD:(j + 1) * HD],
                        lambda a, k: pT[a][:, i % 2, k, :], range(QT)).then_inc(o_mm, 1)

            def project(g, t):
                after(pe, wo_lo, g + 1)
                after(pe, o_lo, 8 * g + B + t // 2 + 1)
                if t >= 2:
                    after(pe, attn_added, 8 * g + t - 1)
                elif isinstance(g, int) and g == NG - 1:
                    pe.wait_ge(gate_ready, 2)
                else:
                    after(pe, v_lo, 8 * (g + 1) + 6 + t + 1)
                product(aux_bank[t % 2][:, :], lambda a, j: oT[a][:, j, t * P:(t + 1) * P],
                        lambda a, j: wos[a][:, j, :], range(2)).then_inc(wo_mm, 1)

            def ffn_weights(n):
                ps = aux_bank[n % 2]
                if n == 0:
                    pe.wait_ge(ffn_in, 16 * (2 + NR))
                if n < 2:
                    pe.wait_ge(attn_added, 8 * (NG - 2) + 6 + n + 1)
                elif n < 6:
                    pe.wait_ge(ffn_lo, n - 1)
                else:
                    pe.wait_ge(ffn_lo, n - 1)
                    pe.wait_ge(gate_w_in, 32)
                if n < 6:
                    for i in range(KT):
                        src = (ffn_raw[:, i, n * P:(n + 1) * P] if n < 4 else
                               (lora_a_raw if n == 4 else lora_b_raw)[:, i * P:(i + 1) * P])
                        last = nc.tensor.transpose(ps[:, i * P:(i + 1) * P], src, ident[:])
                else:
                    for k in range(KT):
                        last = mm(ps[0:B, :], cT[:, k, :], wmod_b[:, k, (n - 6) * D:(n - 5) * D],
                                  start=k == 0, stop=k == KT - 1)
                last.then_inc(ffn_mm, 1)

            scores(0, 0, 0)
            scores(0, 1, 1)
            transposes(0, 0)
            scores(0, 2, 2)

            def pair_b(g):
                first, last = isinstance(g, int) and g == 0, isinstance(g, int) and g == NG - 1
                for i in range(UNITS):
                    u = UNITS * g + i
                    if not (last and i + 1 >= UNITS):
                        transposes(u + 1, (i + 1) % UNITS)
                    if not (last and i + 3 >= UNITS):
                        scores(g + (i + 3) // UNITS, u + 3, (i + 3) % UNITS)
                    if i < B and not first:
                        for t in (2 * i, 2 * i + 1):
                            project(g - 1, t)
                    weigh(g, u, i)
                    if i >= B and not last:
                        for s in (2 * (i - B), 2 * (i - B) + 1):
                            values(g + 1, s)
                    if i >= B and last:
                        for n in (2 * (i - B), 2 * (i - B) + 1):
                            ffn_weights(n)

            loop_peeled(pe, NG, pair_b)

            for t in range(2):
                project(NG - 1, t)

            def h2_transposes(b):
                pe.wait_ge(xn2, 2 * b + 2)
                for half in range(2):
                    n = 2 * b + half
                    after(pe, h2_affine, 2 * (n - 2) + 2)
                    for i in range(2):
                        for q in range(QT):
                            k = 2 * half + i
                            last = nc.tensor.transpose(bank[half][:, i * S + q * P:i * S + (q + 1) * P],
                                                       attn[:, 2 * b + q, k * P:(k + 1) * P], ident[:])
                    last.then_inc(h2_mm, 1)

            def lora_down(b):
                pe.wait_ge(h2_lo, 2 * b + 2)
                after(pe, hl_lo, b - 1)
                product(bank[2 + b % 2][:, 0:S], lambda a, k: aT[a][:, k * P:(k + 1) * P],
                        lambda a, k: hT[a][:, k, b * S:(b + 1) * S], range(KT)).then_inc(hl_mm, 1)

            def ffn(b):
                for t in (2 * b, 2 * b + 1):
                    ps = bank[4 + t % 2]
                    after(pe, out_gated, t - 1)
                    rows = slice(t * P, (t + 1) * P)
                    for k in range(KT):
                        for a, c_ in PARTS:
                            mm(ps[:, :], hT[a][:, k, rows], ffnT[c_][:, k, :], start=k == 0 and a == c_, stop=False)
                    pe.wait_ge(hl_lo, b + 1)
                    for i, (a, c_) in enumerate(PARTS):
                        last = mm(ps[:, :], hlT[a][:, rows], bT[c_], start=False, stop=i == len(PARTS) - 1)
                    last.then_inc(out_mm, 1)

            for b in range(B + 2):
                if b + 1 < B:
                    for t in (2 * b + 2, 2 * b + 3):
                        project(NG - 1, t)
                if b < B:
                    h2_transposes(b)
                if 1 <= b <= B:
                    lora_down(b - 1)
                if b >= 2:
                    ffn(b - 2)


_INS = ["L0_attn_hidden_states", "L0_attn_Wq", "L0_attn_bq", "L0_attn_Wk", "L0_attn_bk", "L0_attn_Wv", "L0_attn_bv",
        "L0_attn_Wo", "L0_attn_bo", "L0_attn_gq", "L0_attn_gk", "L0_ffn_lora_A", "L0_ffn_lora_B", "L0_ffn_W",
        "L0_ffn_bias", "L0_ffn_lora_weights", "L0_c", "L0_wmod"]


def kernel(**inputs):
    import numpy as np
    import concourse.bacc as bacc
    from concourse.bass_utils import run_bass_kernel_spmd

    nc = bacc.Bacc("TRN2", target_bir_lowering=False, num_devices=1)
    arrays, args = {}, []
    for name in _INS:
        a = np.ascontiguousarray(inputs[name])
        arrays[f"in_{name}"] = a
        args.append(nc.dram_tensor(f"in_{name}", a.shape, mybir.dt.from_np(a.dtype), kind="ExternalInput").ap())
    args.append(nc.dram_tensor("out_x", (B, S, D), F32, kind="ExternalOutput").ap())
    adaln_block(nc, *args)
    r = run_bass_kernel_spmd(nc, [arrays], core_ids=[0])
    return r.results[0]["out_x"]
```

```python
import concourse.bass as bass
from concourse import mybir
from concourse.alu_op_type import AluOpType as ALU
from contextlib import ExitStack


F32 = mybir.dt.float32
F32R = mybir.dt.float32r
ACT = mybir.ActivationFunctionType
AX = mybir.AxisListType

B, S, D = 4, 256, 512
H, HD = 32, 128
INNER = H * HD
T = B * S
P = 128
KT = D // P
NT = T // P
QT = S // P
HALF = T // 2
NG = H // 2
UNITS = 2 * B
NU = NG * UNITS
LN_EPS, RMS_EPS = 1e-5, 1e-6
SOFTMAX_SCALE = HD ** -0.5
NR, RANK = 8, 16
LORA_SCALE = 2.0
PARTS = ((0, 0), (0, 1), (1, 0))
SA, CA, GA, SB, CB, GB = range(6)


LAST_PAIR_BEFORE = {4: (1, 2)}
LAST_PAIR_AFTER = {3: (0,), 4: (3, 4)}


def after(eng, sem, n):
    if isinstance(n, int) and n <= 0:
        return
    eng.wait_ge(sem, n)


def loop_peeled(eng, n, body):
    body(0)
    with eng.Fori(1, n - 1) as i:
        body(i)
    body(n - 1)


def adaln_block(nc, x, wq, bq, wk, bk, wv, bv, wo, bo, gq, gk, lora_a, lora_b, w_ffn, b_ffn,
                lora_w, c, wmod, out):
    ctx = ExitStack()
    with ctx:
        def sb(name, shape, dt=F32):
            return ctx.enter_context(nc.sbuf_tensor(name, shape, dt))

        def sem(name):
            return ctx.enter_context(nc.semaphore(name))

        qk_dram = nc.dram_tensor("qk_spill", [H, 2, P, T], F32, kind="Internal").ap()
        gate_dram = nc.dram_tensor("gate_rows", [2, B, D], F32, kind="Internal").ap()

        hT = [sb("hT_hi", [P, KT, T], F32R), sb("hT_lo", [P, KT, T], F32R)]
        attn = sb("attn", [P, NT, D])
        v = [sb("v_hi", [P, NT, 2 * HD], F32R), sb("v_lo", [P, NT, 2 * HD], F32R)]
        wv_raw = sb("wv_raw", [P, KT, 2 * HD])
        wvs = [sb("wv_hi", [P, KT, 2 * HD], F32R), sb("wv_lo", [P, KT, 2 * HD], F32R)]
        wo_raw = sb("wo_raw", [P, 2, D])
        wos = [sb("wo_hi", [P, 2, D], F32R), sb("wo_lo", [P, 2, D], F32R)]
        qk_raw = sb("qk_raw", [P, 2, 2, T])
        qks = [sb("qk_hi", [P, 2, 2, T], F32R), sb("qk_lo", [P, 2, 2, T], F32R)]
        prob = sb("prob", [P, 2, QT, S])
        pT = [sb("pT_hi", [P, 2, QT, S], F32R), sb("pT_lo", [P, 2, QT, S], F32R)]
        oT = [sb("oT_hi", [P, 2, T], F32R), sb("oT_lo", [P, 2, T], F32R)]
        rk = sb("rk", [P, T])
        wstage = sb("wstage", [P, 4096])
        ident = sb("ident", [P, P])
        ones = sb("ones", [P, P])
        vec_rows = sb("vec_rows", [H, 5, HD])
        vec = sb("vec", [P, 5, H])
        vec_now = sb("vec_now", [P, 2, 5])
        c_row = sb("c_row", [B, D])
        silu = sb("silu", [P, 4, KT * B])
        cT = sb("cT", [P, KT, B])
        mod1 = sb("mod1", [P, 2, KT, B])
        mod2 = sb("mod2", [P, 2, KT, B])
        stats = sb("stats", [P, NT, 6])
        mv = sb("mv", [P, NT, 2])
        norm = sb("norm", [P, 4, NT])
        rms = sb("rms", [P, 4, 2 * NT])
        qscale = sb("qscale", [P, 2, NT])
        rowmax = sb("rowmax", [P, 2, QT])
        negmax = sb("negmax", [P, 2, QT])
        rowsum = sb("rowsum", [P, 2, QT])
        rowinv = sb("rowinv", [P, 2, QT])
        lora_coef = sb("lora_coef", [P, 2])
        gate_row = sb("gate_row", [B, 2, D])
        gate_sign = sb("gate_sign", [B, 2, D])

        w_raw = wstage[:, 0:2048].rearrange("p (j w k n) -> p j w k n", j=2, w=2, k=KT)
        ws = [t[:, :, :, 0:D].rearrange("p j w (k n) -> p j w k n", k=KT) for t in qks]
        square = attn[:, 0:4, :]
        sumsq = attn[:, 4:8, :]
        x_sb = qk_raw[:, :, :, :].rearrange("p j w t -> p (j w t)").rearrange("p (n d) -> p n d", n=NT)
        wmod_a = attn[:, :, :].rearrange("p n d -> p (n d)").rearrange("p (k m) -> p k m", k=KT)
        wmod_b = wstage[:, :].rearrange("p (k m) -> p k m", k=KT)
        h_tmp = [prob[:, n, :, :].rearrange("p q s -> p (q s)") for n in range(2)] + [
            rk[:, n * HALF:(n + 1) * HALF] for n in range(2)]
        ffn_raw = [t.rearrange("p (o d) -> p o d", o=2) for t in (
            wv_raw[:, :, :].rearrange("p k n -> p (k n)"), rk[:, :])]
        lora_a_raw, lora_b_raw = x_sb[:, 6, :], x_sb[:, 7, :]
        ffnT = [t[:, 0, :, :].rearrange("p w t -> p (w t)").rearrange("p (k o) -> p k o", k=KT) for t in qks]
        lora_as = [t[:, :, :].rearrange("p k n -> p (k n)")[:, 0:D] for t in wvs]
        bT = [t[:, :, :].rearrange("p k n -> p (k n)")[:, D:2 * D] for t in wvs]
        gates = wstage[:, :].rearrange("p (g b d) -> p g b d", g=2, b=B)
        bias_bc = wo_raw[:, 0, :]
        h2_tmp = prob[:, :, :, :].rearrange("p a q s -> p a (q s)")
        gb_bias = wv_raw[:, :, :].rearrange("p k n -> p (k n)").rearrange("p (a d) -> p a d", a=2)

        bank = [ctx.enter_context(nc.psum_tensor(f"bank{i}", [P, 512], F32)) for i in range(8)]
        s_bank = [bank[0], bank[1]]
        pT_bank = [bank[2], bank[3]]
        o_bank = [bank[4], bank[5]]
        aux_bank = [bank[6], bank[7]]

        x_in = [sem(f"x_in{i}") for i in range(NT // 2)]
        small_in, mod_in = sem("small_in"), sem("mod_in")
        ident_ready, ones_ready = sem("ident_ready"), sem("ones_ready")
        dve_step = sem("dve_step")
        stat_ready, root_ready = sem("stat_ready"), sem("root_ready")
        c_in, c_exp, cT_mm, cT_ready = sem("c_in"), sem("c_exp"), sem("cT_mm"), sem("cT_ready")
        vec_mm, vec_ready = sem("vec_mm"), sem("vec_ready")
        coef_ready = sem("coef_ready")
        vec_now_a, vec_now_b = sem("vec_now_a"), sem("vec_now_b")
        mod_mm, mod_ready = sem("mod_mm"), sem("mod_ready")
        xn_ready, hT_mm, h_affine, hT_hi_ready, hT_lo_ready = (
            sem("xn_ready"), sem("hT_mm"), sem("h_affine"), sem("hT_hi_ready"), sem("hT_lo_ready"))
        w_in = [sem("w_in0"), sem("w_in1")]
        w_hi, w_lo = sem("w_hi"), sem("w_lo")
        proj_mm, squared, summed, scaled = sem("proj_mm"), sem("squared"), sem("summed"), sem("scaled")
        spilled = [sem("spilled0"), sem("spilled1")]
        rms_mm, rms_var, rms_root, rms_cols = sem("rms_mm"), sem("rms_var"), sem("rms_root"), sem("rms_cols")
        rk_mm, rk_ready = sem("rk_mm"), sem("rk_ready")
        wv_in, wo_in, bo_in = sem("wv_in"), sem("wo_in"), sem("bo_in")
        wv_hi, wv_lo, wo_hi, wo_lo = sem("wv_hi_done"), sem("wv_lo_done"), sem("wo_hi_done"), sem("wo_lo_done")
        qk_in = [sem("qk_in0"), sem("qk_in1")]
        k_normed, qk_hi, qk_lo = sem("k_normed"), sem("qk_hi_done"), sem("qk_lo_done")
        score_mm, max_done, negmax_done, exp_done, inv_done, prob_ready = (
            sem("score_mm"), sem("max_done"), sem("negmax_done"), sem("exp_done"), sem("inv_done"), sem("prob_ready"))
        pT_mm, pT_hi, pT_lo = sem("pT_mm"), sem("pT_hi_done"), sem("pT_lo_done")
        o_mm, o_hi, o_lo = sem("o_mm"), sem("o_hi_done"), sem("o_lo_done")
        v_mm, v_hi, v_lo = sem("v_mm"), sem("v_hi_done"), sem("v_lo_done")
        wo_mm, attn_added = sem("wo_mm"), sem("attn_added")
        ffn_in, ffn_mm, ffn_hi, ffn_lo = sem("ffn_in"), sem("ffn_mm"), sem("ffn_hi"), sem("ffn_lo")
        gate_stored, gate_in, bias_in, x_again = (
            sem("gate_stored"), sem("gate_in"), sem("bias_in"), [sem(f"x_again{i}") for i in range(B)])
        gate_mm, lora_in = sem("gate_mm"), sem("lora_in")
        gate_ready, gate_w_in = sem("gate_ready"), sem("gate_w_in")
        attn_gated, x_under, last_gated, x_done = sem("attn_gated"), sem("x_under"), sem("last_gated"), sem("x_done")
        norm2_ready, var2, root2, xn2, h2_mm, h2_affine, h2_hi, h2_lo = (
            sem("norm2_ready"), sem("var2"), sem("root2"), sem("xn2"), sem("h2_mm"), sem("h2_affine"), sem("h2_hi"), sem("h2_lo"))
        lora_hi, lora_lo = sem("lora_hi"), sem("lora_lo")
        bias_gated, x_biased, out_ready_last, out_mm, out_gated, out_ready, stored = (
            sem("bias_gated"), sem("x_biased"), sem("out_ready_last"), sem("out_mm"), sem("out_gated"), sem("out_ready"), sem("stored"))

        x_tiles = x.rearrange("b (q p) d -> p (b q) d", p=P)
        out_tiles = out.rearrange("b (q p) d -> p (b q) d", p=P)
        wmod_t = wmod.rearrange("(k p) m -> p k m", p=P)
        w_t = [w.rearrange("(k p) (h n) -> h p k n", p=P, n=HD) for w in (wq, wk)]
        wv_t = wv.rearrange("(k p) (g n) -> g p k n", p=P, n=2 * HD)
        wo_t = wo.rearrange("(g j p) n -> g p j n", p=P, j=2)

        def at(ap, i):
            if isinstance(i, int):
                return ap[i]
            return ap[bass.ds(i, 1)].rearrange("o ... -> (o ...)") if len(ap.shape) == 1 else drop(ap[bass.ds(i, 1)])

        def drop(ap):
            names = "abcdefg"[:len(ap.shape) - 1]
            return ap.rearrange(f"o {' '.join(names)} -> (o {names[0]}) {' '.join(names[1:])}")

        block = ctx.enter_context(nc.Block())

        @block.sync
        def _(sp):
            sp.dma_start(wmod_a[:, :, :], wmod_t[:, :, 0:2 * D]).then_inc(mod_in, 16)
            for t in range(0, NT, 2):
                sp.dma_start(x_sb[:, t:t + 2, :], x_tiles[:, t:t + 2, :]).then_inc(x_in[t // 2], 16)

            def load_w(h, j):
                for w in range(2):
                    sp.dma_start(w_raw[:, j, w], at(w_t[w], h)).then_inc(w_in[j], 16)

            for j in range(2):
                load_w(j, j)

            def load_qk(g, j):
                for w in (1, 0):
                    sp.dma_start(qk_raw[:, j, w, :], at(qk_dram, 2 * g + j)[w]).then_inc(qk_in[j], 16)

            def pair_a(g):
                for j in range(2):
                    h = 2 * g + j
                    if not (isinstance(g, int) and g == NG - 1):
                        after(sp, w_lo, 2 * h + 2)
                        load_w(h + 2, j)
                    if isinstance(g, int) and h == H - 1:
                        after(sp, spilled[0], 32 * NG)
                        load_qk(0, 0)
                    for w in range(2):
                        after(sp, scaled, 4 * h + 2 * w + 2)
                        sp.dma_start(at(qk_dram, h)[w], qk_raw[:, j, w, :]).then_inc(spilled[j], 16)

            loop_peeled(sp, NG, pair_a)

            after(sp, spilled[1], 32 * NG)
            load_qk(0, 1)
            after(sp, w_lo, 2 * H)
            sp.dma_start(wmod_b[:, :, :], wmod_t[:, :, SB * D:(CB + 1) * D]).then_inc(mod_in, 16)
            after(sp, rms_mm, 1)
            sp.dma_start(attn[:, :, :], bo.rearrange("(a b d) -> a b d", a=1, b=1).to_broadcast([P, NT, D])).then_inc(bo_in, 16)

            def pair_b(g):
                last = isinstance(g, int) and g == NG - 1
                if not last:
                    for j in range(2):
                        after(sp, qk_lo, 2 * (2 * g + j) + 2)
                        load_qk(g + 1, j)
                if isinstance(g, int) and g == 0:
                    after(sp, mod_ready, 4)
                    for i, m in enumerate((GA, GB)):
                        sp.dma_start(wmod_b[:, :, i * D:(i + 1) * D], wmod_t[:, :, m * D:(m + 1) * D]).then_inc(gate_w_in, 16)
                    after(sp, gate_ready, 2)
                    sp.dma_start(gate_dram.rearrange("g b d -> b g d"), gate_row[:, :, :]).then_inc(gate_stored, 16)
                    sp.wait_ge(gate_stored, 16)
                    for g in range(2):
                        sp.dma_start(gates[:, g], gate_dram[g].rearrange("(a b) d -> a b d", a=1).to_broadcast([P, B, D])).then_inc(gate_in, 16)

            loop_peeled(sp, NG, pair_b)

            ffn_tiles = w_ffn.rearrange("(a o p) d -> a p o d", p=P, o=2)
            after(sp, wv_lo, NG)
            sp.dma_start(ffn_raw[0], ffn_tiles[0]).then_inc(ffn_in, 16)

            def load_x(t):
                sp.dma_start(x_sb[:, t:t + 2, :], x_tiles[:, t:t + 2, :]).then_inc(x_again[t // 2], 16)

            after(sp, qk_lo, 2 * (H - 1))
            load_x(0)
            load_x(2)
            after(sp, qk_lo, 2 * H)
            sp.dma_start(lora_a_raw, lora_a.rearrange("n r d -> (n r) d")).then_inc(lora_in, 16)
            for n in range(NR):
                sp.dma_start(lora_b_raw.rearrange("p (o n r) -> p o n r", n=NR, r=RANK)[:, :, n, :],
                             lora_b[n].rearrange("(o p) r -> p o r", p=P)).then_inc(lora_in, 16)
            load_x(4)
            sp.dma_start(ffn_raw[1], ffn_tiles[1]).then_inc(ffn_in, 16)
            after(sp, lora_lo, 1)
            after(sp, ffn_mm, 1)
            load_x(6)
            after(sp, wo_lo, NG)
            sp.dma_start(bias_bc, b_ffn.rearrange("(a d) -> a d", a=1).to_broadcast([P, D])).then_inc(bias_in, 16)
            for t in range(NT):
                if t < 6:
                    after(sp, out_ready, t + 1)
                else:
                    after(sp, out_ready_last, t - 5)
                sp.dma_start(out_tiles[:, t, :], attn[:, t, :]).then_inc(stored, 16)
            sp.wait_ge(stored, 16 * NT)

        @block.gpsimd
        def _(pool):
            nc.gpsimd.memset(ones[:], 1.0).then_inc(ones_ready, 1)
            nc.gpsimd.memset(ident[:], 0.0).then_inc(ident_ready, 1)
            pool.wait_ge(ident_ready, 1)
            nc.gpsimd.affine_select(out=ident[:], in_=ident[:], compare_op=ALU.not_equal, fill=1.0, base=0,
                                    pattern=[[-1, P]], channel_multiplier=1).then_inc(ident_ready, 1)
            pool.dma_start(wv_raw[:, :, :], wv_t[0]).then_inc(wv_in, 16)
            pool.dma_start(wo_raw[:, :, :], wo_t[0]).then_inc(wo_in, 16)

            def pair_a(g):
                for j in range(2):
                    h = 2 * g + j
                    for s in range(4):
                        after(pool, squared, 4 * h + s + 1)
                        after(pool, summed, 4 * h - 4 + s + 1)
                        if isinstance(g, int) and h == 0:
                            nc.gpsimd.tensor_copy(sumsq[:, s], square[:, s]).then_inc(summed, 1)
                        else:
                            nc.gpsimd.tensor_tensor(sumsq[:, s], sumsq[:, s], square[:, s], ALU.add).then_inc(summed, 1)

            def split_lo(dst, raw, hi, done):
                nc.gpsimd.tensor_tensor(dst, raw, hi.bitcast(F32), ALU.subtract).then_inc(done, 1)

            def norm_k(g, j):
                after(pool, qk_in[j], 32 * (g + 1))
                nc.gpsimd.tensor_tensor(qk_raw[:, j, 1, :], qk_raw[:, j, 1, :], rk[:, :], ALU.mult).then_inc(k_normed, 1)

            def lo_qk(g, j, parts=(0, 1)):
                for w in parts:
                    after(pool, qk_hi, 2 * (2 * g + j) + w + 1)
                    split_lo(qks[1][:, j, w, :], qk_raw[:, j, w, :], qks[0][:, j, w, :], qk_lo)

            def lo_wv(g):
                after(pool, wv_hi, g + 1)
                split_lo(wvs[1][:, :, :], wv_raw[:, :, :], wvs[0][:, :, :], wv_lo)

            def lo_wo(g):
                after(pool, wo_hi, g + 1)
                split_lo(wos[1][:, :, :], wo_raw[:, :, :], wos[0][:, :, :], wo_lo)

            lo_wv(0)
            loop_peeled(pool, NG, pair_a)
            lo_qk(0, 0, (0,))
            pool.wait_ge(k_normed, 1)
            norm_k(0, 1)
            pool.wait_ge(qk_lo, 2)
            lo_qk(0, 1)

            def pair_b(g):
                last = isinstance(g, int) and g == NG - 1
                if not last:
                    after(pool, wv_lo, g + 1)
                    pool.dma_start(wv_raw[:, :, :], at(wv_t, g + 1)).then_inc(wv_in, 16)
                    norm_k(g + 1, 0)
                    lo_wv(g + 1)
                    lo_qk(g + 1, 0)
                if last:
                    pool.wait_ge(lora_hi, 1)
                    split_lo(lora_as[1], lora_a_raw, lora_as[0], lora_lo)
                    pool.wait_ge(gate_in, 32)
                    for t in range(6):
                        x_and_attn(t)
                lo_wo(g)
                if not last:
                    after(pool, wo_lo, g + 1)
                    pool.dma_start(wo_raw[:, :, :], at(wo_t, g + 1)).then_inc(wo_in, 16)
                    norm_k(g + 1, 1)
                    lo_qk(g + 1, 1)

            def x_and_attn(t):
                pool.wait_ge(attn_added, 8 * (NG - 2) + t + 1)
                nc.gpsimd.tensor_tensor(attn[:, t], attn[:, t], gates[:, 0, t // QT], ALU.mult).then_inc(attn_gated, 1)
                pool.wait_ge(attn_gated, t + 1)
                pool.wait_ge(x_again[t // 2], 16)
                nc.gpsimd.tensor_tensor(attn[:, t], attn[:, t], x_sb[:, t, :], ALU.add).then_inc(x_under, 1)

            loop_peeled(pool, NG, pair_b)

            for t in range(6, NT):
                x_and_attn(t)
            pool.wait_ge(bias_in, 16)
            pool.wait_ge(ffn_mm, 5)
            for b in range(B):
                after(pool, x_biased, 2 * b - 2)
                nc.gpsimd.tensor_tensor(gb_bias[:, b % 2], gates[:, 1, b], bias_bc, ALU.mult).then_inc(bias_gated, 1)
                pool.wait_ge(bias_gated, b + 1)
                for t in (2 * b, 2 * b + 1):
                    pool.wait_ge(xn2, t + 1)
                    nc.gpsimd.tensor_tensor(x_sb[:, t], x_sb[:, t], gb_bias[:, b % 2], ALU.add).then_inc(x_biased, 1)
                if b >= 1:
                    for t in (2 * b - 2, 2 * b - 1):
                        pool.wait_ge(x_biased, t + 1)
                        pool.wait_ge(out_gated, t + 1)
                        nc.gpsimd.tensor_tensor(attn[:, t], attn[:, t], x_sb[:, t], ALU.add).then_inc(out_ready, 1)

        @block.scalar
        def _(act):
            act.dma_start(c_row[:, :], c).then_inc(c_in, 16)
            for i, a in enumerate((bq, bk, gq, gk, bv)):
                act.dma_start(vec_rows[:, i, :], a.rearrange("(h n) -> h n", n=HD)).then_inc(small_in, 16)
            lw = lora_w.rearrange("(n a b) -> n a b", a=1, b=1)
            act.dma_start(lora_coef[:, 0:1], lw.to_broadcast([NR, RANK, 1])).then_inc(small_in, 16)

            act.wait_ge(cT_mm, 1)
            nc.scalar.activation(silu[:, 1, :], bank[0][:, 0:KT * B], ACT.Exp, scale=-1.0).then_inc(c_exp, 1)
            for half in range(2):
                act.wait_ge(stat_ready, half + 1)
                nc.scalar.activation(norm[:, 1, 4 * half:4 * half + 4], norm[:, 0, 4 * half:4 * half + 4], ACT.Sqrt).then_inc(root_ready, 1)

            for n in range(2 * KT):
                half, k = divmod(n, KT)
                act.wait_ge(hT_mm, n + 1)
                if n == 0:
                    act.wait_ge(mod_ready, 2)
                if n >= 4:
                    act.wait_ge(hT_lo_ready, n - 3)
                for i in range(2):
                    b = 2 * half + i
                    nc.scalar.activation(h_tmp[n % 4][:, i * S:(i + 1) * S], bank[n][:, i * S:(i + 1) * S], ACT.Identity,
                                         scale=mod1[:, 1, k, b:b + 1], bias=mod1[:, 0, k, b:b + 1]).then_inc(h_affine, 1)

            def pair_a(g):
                for j in range(2):
                    h = 2 * g + j
                    for s in range(4):
                        w = s // 2
                        after(act, proj_mm, 4 * h + s + 1)
                        after(act, summed, 4 * h - 4 + s + 1)
                        if s == 0:
                            after(act, vec_now_a, h + 1)
                        nc.scalar.activation(square[:, s], bank[4 * j + s][:, :], ACT.Square,
                                             bias=vec_now[:, j, w:w + 1]).then_inc(squared, 1)

            def hi_copy(dst, src, done):
                nc.scalar.activation(dst, src, ACT.Copy).then_inc(done, 1)

            def hi_wv(g):
                after(act, wv_in, 16 * (g + 1))
                after(act, v_mm, 8 * g)
                hi_copy(wvs[0][:, :, :], wv_raw[:, :, :], wv_hi)

            def hi_wo(g):
                after(act, wo_in, 16 * (g + 1))
                after(act, wo_mm, 8 * g)
                hi_copy(wos[0][:, :, :], wo_raw[:, :, :], wo_hi)

            def hi_qk(g, j, w):
                h = 2 * g + j
                if w:
                    after(act, k_normed, h + 1)
                else:
                    after(act, qk_in[j], 32 * (g + 1))
                after(act, score_mm, 4 * (h - 1))
                if isinstance(g, int) and g == 0:
                    act.wait_ge(proj_mm, 4 * (H - 1 + j))
                hi_copy(qks[0][:, j, w, :], qk_raw[:, j, w, :], qk_hi)

            def hi_v(n, s):
                after(act, v_mm, n + 1)
                hi_copy(v[0][:, s, :], aux_bank[s % 2][:, 0:2 * HD], v_hi)

            def exp(g, u, i):
                b = i % B
                after(act, negmax_done, u + 1)
                after(act, pT_mm, u - 1)
                for q in range(QT):
                    t = QT * b + q
                    nc.scalar.activation(prob[:, i % 2, q, :], s_bank[i % 2][:, q * S:(q + 1) * S], ACT.Exp,
                                         scale=qscale[:, 0, t:t + 1], bias=negmax[:, i % 2, q:q + 1],
                                         accum_out=rowsum[:, i % 2, q:q + 1]).then_inc(exp_done, 1)

            def hi_pT(u, i):
                after(act, pT_mm, u + 1)
                after(act, o_mm, u - 1)
                hi_copy(pT[0][:, i % 2, :, :], pT_bank[i % 2][:, :].rearrange("p (k q) -> p k q", k=QT), pT_hi)

            def hi_o(u, i, h):
                j, b = divmod(i, B)
                after(act, o_mm, u + 1)
                if b == 0:
                    after(act, vec_now_b, h + 1)
                nc.scalar.activation(oT[0][:, j, b * S:(b + 1) * S], o_bank[i % 2][:, 0:S], ACT.Identity,
                                     bias=vec_now[:, j, 4:5]).then_inc(o_hi, 1)

            def root(b):
                act.wait_ge(var2, b + 1)
                nc.scalar.activation(norm[:, 1, 2 * b:2 * b + 2], norm[:, 0, 2 * b:2 * b + 2], ACT.Sqrt).then_inc(root2, 1)

            def apply_norm(b):
                act.wait_ge(norm2_ready, b + 1)
                for t in (2 * b, 2 * b + 1):
                    nc.scalar.activation(attn[:, t, :], x_sb[:, t, :], ACT.Identity, scale=norm[:, 2, t:t + 1],
                                         bias=norm[:, 3, t:t + 1]).then_inc(xn2, 1)

            hi_wv(0)
            loop_peeled(act, NG, pair_a)

            hi_qk(0, 0, 0)
            for s in range(2):
                hi_v(s, s)
            act.wait_ge(rms_var, 1)
            nc.scalar.activation(rms[:, 1, :], rms[:, 0, :], ACT.Sqrt).then_inc(rms_root, 1)
            for s in range(2, 4):
                hi_v(s, s)
            hi_qk(0, 0, 1)
            for s in range(4, NT):
                hi_v(s, s)
            hi_qk(0, 1, 0)
            hi_qk(0, 1, 1)
            exp(0, 0, 0)
            exp(0, 1, 1)
            hi_pT(0, 0)
            exp(0, 2, 2)

            def pair_b(g):
                first, last = isinstance(g, int) and g == 0, isinstance(g, int) and g == NG - 1
                for i in range(UNITS):
                    u = UNITS * g + i
                    if not (last and i + 1 >= UNITS):
                        hi_pT(u + 1, (i + 1) % UNITS)
                    if i == 0 and not last:
                        hi_wv(g + 1)
                    if i in (1, 2) and not last:
                        hi_qk(g + 1, 0, i - 1)
                    if i == 4:
                        hi_wo(g)
                    if i in (5, 6) and not last:
                        hi_qk(g + 1, 1, i - 5)
                    if not (last and i + 3 >= UNITS):
                        exp(g, u + 3, (i + 3) % UNITS)
                    hi_o(u, i, 2 * g + i // B)
                    if i >= B and not last:
                        for t in range(2):
                            s = 2 * (i - B) + t
                            hi_v(8 * (g + 1) + s, s)
                    if last:
                        if i == 0:
                            act.wait_ge(lora_in, 16 * (1 + NR))
                            act.wait_ge(v_mm, 8 * NG)
                            hi_copy(lora_as[0], lora_a_raw, lora_hi)
                        for n in LAST_PAIR_BEFORE.get(i, ()) + LAST_PAIR_AFTER.get(i, ()):
                            hi_ffn(n)
                        if i > B + 1:
                            root(i - B - 2)
                        if i == UNITS - 1:
                            apply_norm(0)

            def hi_ffn(n):
                act.wait_ge(ffn_mm, n + 1)
                if n == 0:
                    act.wait_ge(coef_ready, 1)
                    nc.scalar.activation(bT[0], aux_bank[0][:, :], ACT.Copy, scale=lora_coef[:, 1:2]).then_inc(ffn_hi, 1)
                else:
                    hi_copy(ffnT[0][:, n - 1, :], aux_bank[n % 2][:, :], ffn_hi)

            loop_peeled(act, NG, pair_b)

            def affine(b):
                for half in range(2):
                    n = 2 * b + half
                    act.wait_ge(h2_mm, n + 1)
                    after(act, h2_lo, n - 1)
                    for i in range(2):
                        k = 2 * half + i
                        nc.scalar.activation(h2_tmp[:, n % 2, i * S:(i + 1) * S], bank[half][:, i * S:(i + 1) * S],
                                             ACT.Identity, scale=mod2[:, 1, k, b:b + 1],
                                             bias=mod2[:, 0, k, b:b + 1]).then_inc(h2_affine, 1)
                    act.wait_ge(h2_affine, 2 * n + 2)
                    nc.scalar.activation(hT[0][:, 2 * half:2 * half + 2, b * S:(b + 1) * S],
                                         h2_tmp[:, n % 2, :].rearrange("p (k t) -> p k t", k=2), ACT.Copy).then_inc(h2_hi, 1)

            affine(0)
            root(2)
            apply_norm(1)
            apply_norm(2)
            root(3)
            affine(1)
            apply_norm(3)
            affine(2)
            affine(3)

        @block.vector
        def _(dve):
            steps = [0]

            def link(ins):
                steps[0] += 1
                ins.then_inc(dve_step, 1)
                dve.wait_ge(dve_step, steps[0])

            def newton(y, var, tmp):
                link(nc.vector.tensor_tensor(tmp, y, y, ALU.mult))
                link(nc.vector.tensor_tensor(tmp, tmp, var, ALU.mult))
                link(nc.vector.tensor_scalar(tmp, tmp, -0.5, 1.5, ALU.mult, ALU.add))
                return nc.vector.tensor_tensor(y, y, tmp, ALU.mult)

            dve.wait_ge(c_exp, 1)
            link(nc.vector.tensor_copy(silu[:, 0, :], bank[0][:, 0:KT * B]))
            link(nc.vector.tensor_scalar(silu[:, 2, :], silu[:, 1, :], 1.0, None, ALU.add))
            link(nc.vector.reciprocal(silu[:, 3, :], silu[:, 2, :]))
            nc.vector.tensor_tensor(cT[:, :, :].rearrange("p k b -> p (k b)"), silu[:, 0, :], silu[:, 3, :],
                                    ALU.mult).then_inc(cT_ready, 1)
            dve.wait_ge(small_in, 96)
            nc.vector.tensor_scalar(lora_coef[:, 1:2], lora_coef[:, 0:1], LORA_SCALE, None, ALU.mult).then_inc(coef_ready, 1)

            def modulation(dst, ps, n):
                cols = ps[:, 0:2 * KT * B].rearrange("p (m k b) -> p m k b", m=2, k=KT)
                dve.wait_ge(mod_mm, n + 1)
                nc.vector.tensor_copy(dst[:, 0], cols[:, 0]).then_inc(mod_ready, 1)
                nc.vector.tensor_scalar(dst[:, 1], cols[:, 1], 1.0, None, ALU.add).then_inc(mod_ready, 1)

            def start_norm(half):
                four = slice(4 * half, 4 * half + 4)
                for t in range(4 * half, 4 * half + 4):
                    if t % 2 == 0:
                        dve.wait_ge(x_in[t // 2], 16)
                    last = nc.vector.bn_stats(stats[:, t, :], x_sb[:, t, :])
                link(last)
                for t in range(4 * half, 4 * half + 4):
                    last = nc.vector.bn_aggr(mv[:, t, :], stats[:, t, :])
                link(last)
                nc.vector.tensor_scalar(norm[:, 0, four], mv[:, four, 1], LN_EPS, None, ALU.add).then_inc(stat_ready, 1)
                dve.wait_ge(root_ready, half + 1)
                link(nc.vector.reciprocal(norm[:, 2, four], norm[:, 1, four]))
                link(newton(norm[:, 2, four], norm[:, 0, four], norm[:, 3, four]))
                for t in range(4 * half, 4 * half + 4):
                    nc.vector.tensor_scalar(x_sb[:, t, :], x_sb[:, t, :], mv[:, t, 0:1], norm[:, 2, t:t + 1],
                                            ALU.subtract, ALU.mult).then_inc(xn_ready, 1)

            for half in range(2):
                start_norm(half)

            def split_w(g, j):
                h = 2 * g + j
                after(dve, w_in[j], 32 * (g + 1))
                after(dve, proj_mm, 4 * (h - 1))
                for w in range(2):
                    nc.vector.tensor_copy(ws[0][:, j, w], w_raw[:, j, w]).then_inc(w_hi, 1)
                for w in range(2):
                    after(dve, w_hi, 2 * h + w + 1)
                    nc.vector.tensor_tensor(ws[1][:, j, w], w_raw[:, j, w], ws[0][:, j, w].bitcast(F32),
                                            ALU.subtract).then_inc(w_lo, 1)

            def take_vectors(h, j, done):
                src = vec[:, :, h:h + 1] if isinstance(h, int) else vec[:, :, bass.ds(h, 1)]
                nc.vector.tensor_scalar(vec_now[:, j, :], src.rearrange("p a o -> p (a o)"), 1.0, None, ALU.mult).then_inc(done, 1)


            split_w(0, 0)
            modulation(mod1, bank[1], 0)
            dve.wait_ge(vec_mm, 1)
            nc.vector.tensor_copy(vec[:, :, :], bank[2][:, 0:5 * H].rearrange("p (a h) -> p a h", a=5)).then_inc(vec_ready, 1)
            dve.wait_ge(vec_ready, 1)

            for n in range(2 * KT):
                half, k = divmod(n, KT)
                dve.wait_ge(h_affine, 2 * n + 2)
                hi = hT[0][:, k, half * HALF:(half + 1) * HALF]
                nc.vector.tensor_copy(hi, h_tmp[n % 4]).then_inc(hT_hi_ready, 1)
                dve.wait_ge(hT_hi_ready, n + 1)
                nc.vector.tensor_tensor(hT[1][:, k, half * HALF:(half + 1) * HALF], h_tmp[n % 4], hi.bitcast(F32),
                                        ALU.subtract).then_inc(hT_lo_ready, 1)

            def pair_a(g):
                for j in range(2):
                    h = 2 * g + j
                    if j == 0:
                        split_w(g, 1)
                    elif not (isinstance(g, int) and g == NG - 1):
                        split_w(g + 1, 0)
                    after(dve, squared, 4 * (h - 1))
                    take_vectors(h, j, vec_now_a)
                    after(dve, spilled[j], 32 * g)
                    after(dve, vec_now_a, h + 1)
                    for s in range(4):
                        w, half = divmod(s, 2)
                        after(dve, squared, 4 * h + s + 1)
                        nc.vector.tensor_scalar(qk_raw[:, j, w, half * HALF:(half + 1) * HALF], bank[4 * j + s][:, :],
                                                vec_now[:, j, w:w + 1], vec_now[:, j, 2 + w:3 + w],
                                                ALU.add, ALU.mult).then_inc(scaled, 1)

            loop_peeled(dve, NG, pair_a)

            def lo_v(n, s):
                after(dve, v_hi, n + 1)
                nc.vector.tensor_tensor(v[1][:, s, :], aux_bank[s % 2][:, 0:2 * HD], v[0][:, s, :].bitcast(F32),
                                        ALU.subtract).then_inc(v_lo, 1)

            for s in range(2):
                lo_v(s, s)
            dve.wait_ge(rms_mm, 1)
            nc.vector.tensor_scalar(rms[:, 0, :], bank[2][:, 0:2 * NT], 1.0 / INNER, RMS_EPS, ALU.mult, ALU.add).then_inc(rms_var, 1)
            dve.wait_ge(rms_root, 1)
            link(nc.vector.reciprocal(rms[:, 2, :], rms[:, 1, :]))
            newton(rms[:, 2, :], rms[:, 0, :], rms[:, 3, :]).then_inc(rms_cols, 1)
            dve.wait_ge(rms_cols, 1)
            nc.vector.tensor_scalar(qscale[:, 0, :], rms[:, 2, 0:NT], SOFTMAX_SCALE, None, ALU.mult)
            nc.vector.tensor_scalar(qscale[:, 1, :], rms[:, 2, 0:NT], -SOFTMAX_SCALE, None, ALU.mult)
            for s in range(2, 4):
                lo_v(s, s)
            dve.wait_ge(rk_mm, 1)
            for i in range(2):
                nc.vector.tensor_copy(rk[:, i * HALF:(i + 1) * HALF], bank[i][:, :]).then_inc(rk_ready, 1)
            dve.wait_ge(qk_in[0], 32)
            dve.wait_ge(rk_ready, 2)
            nc.vector.tensor_tensor(qk_raw[:, 0, 1, :], qk_raw[:, 0, 1, :], rk[:, :], ALU.mult).then_inc(k_normed, 1)
            for s in range(4, 6):
                lo_v(s, s)
            dve.wait_ge(qk_hi, 2)
            nc.vector.tensor_tensor(qks[1][:, 0, 1, :], qk_raw[:, 0, 1, :], qks[0][:, 0, 1, :].bitcast(F32),
                                    ALU.subtract).then_inc(qk_lo, 1)
            for s in range(6, NT):
                lo_v(s, s)

            def maxima(u, i):
                b = i % B
                after(dve, score_mm, u + 1)
                nc.vector.tensor_reduce(rowmax[:, i % 2, :], s_bank[i % 2][:, :].rearrange("p (q s) -> p q s", q=QT),
                                        AX.X, ALU.max).then_inc(max_done, 1)
                after(dve, max_done, u + 1)
                nc.vector.tensor_tensor(negmax[:, i % 2, :], rowmax[:, i % 2, :], qscale[:, 1, QT * b:QT * (b + 1)],
                                        ALU.mult).then_inc(negmax_done, 1)

            def normalise(u, i):
                after(dve, exp_done, QT * (u + 1))
                nc.vector.reciprocal(rowinv[:, i % 2, :], rowsum[:, i % 2, :]).then_inc(inv_done, 1)
                after(dve, inv_done, u + 1)
                for q in range(QT):
                    last = nc.vector.tensor_scalar(prob[:, i % 2, q, :], prob[:, i % 2, q, :], rowinv[:, i % 2, q:q + 1],
                                                   None, ALU.mult)
                last.then_inc(prob_ready, 1)

            def lo_pT(u, i):
                after(dve, pT_hi, u + 1)
                nc.vector.tensor_tensor(pT[1][:, i % 2, :, :], pT_bank[i % 2][:, :].rearrange("p (k q) -> p k q", k=QT),
                                        pT[0][:, i % 2, :, :].bitcast(F32), ALU.subtract).then_inc(pT_lo, 1)

            def lo_o(u, i, h):
                j, b = divmod(i, B)
                after(dve, o_hi, u + 1)
                after(dve, vec_now_b, h + 1)
                nc.vector.scalar_tensor_tensor(out=oT[1][:, j, b * S:(b + 1) * S], in0=o_bank[i % 2][:, 0:S],
                                               scalar=vec_now[:, j, 4:5], in1=oT[0][:, j, b * S:(b + 1) * S].bitcast(F32),
                                               op0=ALU.add, op1=ALU.subtract).then_inc(o_lo, 1)

            def add_attn(g, t):
                after(dve, wo_mm, 8 * g + t + 1)
                nc.vector.tensor_tensor(attn[:, t, :], aux_bank[t % 2][:, :], attn[:, t, :], ALU.add).then_inc(attn_added, 1)

            def residual(b):
                two = (2 * b, 2 * b + 1)
                for t in two:
                    dve.wait_ge(wo_mm, 8 * (NG - 1) + t + 1)
                    dve.wait_ge(x_under, t + 1)
                    nc.vector.tensor_tensor(x_sb[:, t, :], aux_bank[t % 2][:, :], gates[:, 0, b, :], ALU.mult).then_inc(last_gated, 1)
                for t in two:
                    dve.wait_ge(last_gated, t + 1)
                    nc.vector.tensor_tensor(x_sb[:, t, :], x_sb[:, t, :], attn[:, t, :], ALU.add).then_inc(x_done, 1)
                for t in two:
                    dve.wait_ge(x_done, t + 1)
                    last = nc.vector.bn_stats(stats[:, t, :], x_sb[:, t, :])
                link(last)
                for t in two:
                    last = nc.vector.bn_aggr(mv[:, t, :], stats[:, t, :])
                link(last)
                nc.vector.tensor_scalar(norm[:, 0, 2 * b:2 * b + 2], mv[:, 2 * b:2 * b + 2, 1], LN_EPS, None, ALU.add).then_inc(var2, 1)

            def norm_factors(b):
                two = slice(2 * b, 2 * b + 2)
                dve.wait_ge(root2, b + 1)
                link(nc.vector.reciprocal(norm[:, 2, two], norm[:, 1, two]))
                link(newton(norm[:, 2, two], norm[:, 0, two], norm[:, 3, two]))
                nc.vector.scalar_tensor_tensor(out=norm[:, 3, two], in0=mv[:, two, 0], scalar=-1.0, in1=norm[:, 2, two],
                                               op0=ALU.mult, op1=ALU.mult).then_inc(norm2_ready, 1)

            maxima(0, 0)
            maxima(1, 1)
            normalise(0, 0)
            normalise(1, 1)
            lo_pT(0, 0)
            maxima(2, 2)
            normalise(2, 2)

            def pair_b(g):
                first, last = isinstance(g, int) and g == 0, isinstance(g, int) and g == NG - 1
                for i in range(UNITS):
                    u = UNITS * g + i
                    if not (last and i + 1 >= UNITS):
                        lo_pT(u + 1, (i + 1) % UNITS)
                    if not (last and i + 3 >= UNITS):
                        maxima(u + 3, (i + 3) % UNITS)
                    if i < B and not first:
                        for t in (2 * i, 2 * i + 1):
                            add_attn(g - 1, t)
                    if not (last and i + 3 >= UNITS):
                        normalise(u + 3, (i + 3) % UNITS)
                    if i % B == 0:
                        after(dve, o_hi, UNITS * (g - 1) + i + B)
                        take_vectors(2 * g + i // B, i // B, vec_now_b)
                    lo_o(u, i, 2 * g + i // B)
                    if i >= B and not last:
                        for s in (2 * (i - B), 2 * (i - B) + 1):
                            lo_v(8 * (g + 1) + s, s)
                    if first and i == B - 1:
                        modulation(mod2, aux_bank[0], 1)
                        dve.wait_ge(bo_in, 16)
                    if first and i == UNITS - 1:
                        clamp_gates()
                    if last:
                        for n in LAST_PAIR_BEFORE.get(i, ()) + LAST_PAIR_AFTER.get(i, ()):
                            lo_ffn(n)
                        if i > B + 1:
                            norm_factors(i - B - 2)
                        if i > B:
                            residual(i - B - 1)

            def lo_ffn(n):
                ps = aux_bank[n % 2]
                dve.wait_ge(ffn_hi, n + 1)
                if n == 0:
                    nc.vector.scalar_tensor_tensor(out=bT[1], in0=ps[:, :], scalar=lora_coef[:, 1:2], in1=bT[0].bitcast(F32),
                                                   op0=ALU.mult, op1=ALU.subtract).then_inc(ffn_lo, 1)
                else:
                    nc.vector.tensor_tensor(ffnT[1][:, n - 1, :], ps[:, :], ffnT[0][:, n - 1, :].bitcast(F32),
                                            ALU.subtract).then_inc(ffn_lo, 1)

            def clamp_gates():
                for m in range(2):
                    ps = aux_bank[m][0:B, :]
                    dve.wait_ge(gate_mm, m + 1)
                    link(nc.vector.tensor_scalar(gate_sign[:, m, :], ps, 0.0, 2.0, ALU.is_ge, ALU.mult))
                    link(nc.vector.tensor_scalar(gate_sign[:, m, :], gate_sign[:, m, :], 1.0, None, ALU.subtract))
                    link(nc.vector.tensor_tensor(gate_row[:, m, :], ps, gate_sign[:, m, :], ALU.mult))
                    nc.vector.scalar_tensor_tensor(out=gate_row[:, m, :], in0=gate_row[:, m, :], scalar=0.25,
                                                   in1=gate_sign[:, m, :], op0=ALU.max, op1=ALU.mult).then_inc(gate_ready, 1)

            loop_peeled(dve, NG, pair_b)

            def lo_h2(b):
                for half in range(2):
                    n = 2 * b + half
                    dve.wait_ge(h2_hi, n + 1)
                    part = (slice(None), slice(2 * half, 2 * half + 2), slice(b * S, (b + 1) * S))
                    nc.vector.tensor_tensor(hT[1][part], h2_tmp[:, n % 2, :].rearrange("p (k t) -> p k t", k=2),
                                            hT[0][part].bitcast(F32), ALU.subtract).then_inc(h2_lo, 1)

            def finish(b):
                for t in (2 * b, 2 * b + 1):
                    dve.wait_ge(out_mm, t + 1)
                    nc.vector.tensor_tensor(attn[:, t, :], bank[4 + t % 2][:, :], gates[:, 1, b, :], ALU.mult).then_inc(out_gated, 1)
                    if t >= 6:
                        dve.wait_ge(out_gated, t + 1)
                        dve.wait_ge(x_biased, t + 1)
                        nc.vector.tensor_tensor(attn[:, t, :], attn[:, t, :], x_sb[:, t, :], ALU.add).then_inc(out_ready_last, 1)

            lo_h2(0)
            residual(3)
            norm_factors(2)
            lo_h2(1)
            norm_factors(3)
            finish(0)
            lo_h2(2)
            finish(1)
            lo_h2(3)
            finish(2)
            finish(3)

        @block.tensor
        def _(pe):
            mm = nc.tensor.matmul

            def product(out_, lhs, rhs, steps):
                n = len(steps) * len(PARTS)
                for i, (k, (a, b)) in enumerate([(k, p) for k in steps for p in PARTS]):
                    last = mm(out_, lhs(a, k), rhs(b, k), start=i == 0, stop=i == n - 1)
                return last

            pe.wait_ge(ident_ready, 2)
            pe.wait_ge(c_in, 16)
            for k in range(KT):
                last = nc.tensor.transpose(bank[0][:, k * B:(k + 1) * B], c_row[:, k * P:(k + 1) * P], ident[0:B, 0:B])
            last.then_inc(cT_mm, 1)
            pe.wait_ge(small_in, 96)
            for i in range(5):
                last = nc.tensor.transpose(bank[2][:, i * H:(i + 1) * H], vec_rows[:, i, :], ident[0:H, 0:H])
            last.then_inc(vec_mm, 1)

            def mod_columns(ps, w, tiles=range(2 * KT)):
                for m in tiles:
                    for k in range(KT):
                        last = mm(ps[:, m * B:(m + 1) * B], w[:, k, m * P:(m + 1) * P], cT[:, k, :],
                                  start=k == 0, stop=k == KT - 1)
                return last

            def x_transposes(n):
                half, k = divmod(n, KT)
                pe.wait_ge(xn_ready, 4 * half + 4)
                for t in range(4):
                    last = nc.tensor.transpose(bank[n][:, t * P:(t + 1) * P], x_sb[:, 4 * half + t, k * P:(k + 1) * P], ident[:])
                last.then_inc(hT_mm, 1)

            pe.wait_ge(cT_ready, 1)
            pe.wait_ge(mod_in, 16)
            mod_columns(bank[1], wmod_a).then_inc(mod_mm, 1)
            x_transposes(0)
            pe.wait_ge(mod_ready, 2)
            x_transposes(1)
            pe.wait_ge(vec_ready, 1)
            for n in range(2, 2 * KT):
                x_transposes(n)

            def pair_a(g):
                for j in range(2):
                    h = 2 * g + j
                    for w in range(2):
                        after(pe, w_lo, 2 * h + w + 1)
                        after(pe, scaled, 4 * (h - 2) + 2 * w + 2)
                        steps = [(k, i, half) for k in range(KT) for i in range(len(PARTS)) for half in range(2)]
                        if isinstance(g, int) and h == 0:
                            steps.sort(key=lambda step: step[2])
                        for k, i, half in steps:
                            a, b = PARTS[i]
                            if isinstance(g, int) and h == 0 and w == 0:
                                pe.wait_ge(hT_lo_ready, KT * half + k + 1)
                            done = k == KT - 1 and i == len(PARTS) - 1
                            last = mm(bank[4 * j + 2 * w + half][:, :], ws[a][:, j, w, k, :],
                                      hT[b][:, k, half * HALF:(half + 1) * HALF],
                                      start=k == 0 and i == 0, stop=done)
                            if done:
                                last.then_inc(proj_mm, 1)

            loop_peeled(pe, NG, pair_a)

            def values(g, s):
                n = 8 * g + s
                after(pe, wv_lo, g + 1)
                if s == 0 and isinstance(g, int) and g == 1:
                    pe.wait_ge(mod_ready, 4)
                if s < 2 and isinstance(g, int) and g == 0:
                    pe.wait_ge(scaled, 4 * H)
                elif s >= 2 or (isinstance(g, int) and g == 1):
                    after(pe, v_lo, n - 1)
                else:
                    after(pe, attn_added, 8 * (g - 2) + 6 + s + 1)
                product(aux_bank[s % 2][:, 0:2 * HD], lambda a, k: hT[a][:, k, s * P:(s + 1) * P],
                        lambda b, k: wvs[b][:, k, :], range(KT)).then_inc(v_mm, 1)

            for s in range(2):
                values(0, s)
            for t in range(2 * NT):
                if t % 4 == 0:
                    pe.wait_ge(summed, 4 * (H - 1) + t // 4 + 1)
                last = mm(bank[2][:, t:t + 1], sumsq[:, t // 4, (t % 4) * P:(t % 4 + 1) * P], ones[:, 0:1], start=True, stop=True)
            last.then_inc(rms_mm, 1)
            for s in range(2, 4):
                values(0, s)
            pe.wait_ge(rms_cols, 1)
            for t in range(NT):
                last = mm(bank[t // 4][:, (t % 4) * P:(t % 4 + 1) * P], rms[:, 2, NT + t:NT + t + 1].to_broadcast([P, P]),
                          ident[:], start=True, stop=True)
            last.then_inc(rk_mm, 1)
            for s in range(4, NT):
                values(0, s)

            def scores(g, u, i):
                j, b = divmod(i, B)
                if b == 0:
                    after(pe, qk_lo, 2 * (2 * g + j) + 2)
                for q in range(QT):
                    rows = slice(b * S + q * P, b * S + (q + 1) * P)
                    last = product(s_bank[i % 2][:, q * S:(q + 1) * S], lambda a, _: qks[a][:, j, 0, rows],
                                   lambda a, _: qks[a][:, j, 1, b * S:(b + 1) * S], [0])
                last.then_inc(score_mm, 1)

            def transposes(u, i):
                after(pe, prob_ready, u + 1)
                after(pe, pT_lo, u - 1)
                for k in range(QT):
                    for q in range(QT):
                        last = nc.tensor.transpose(pT_bank[i % 2][:, k * S + q * P:k * S + (q + 1) * P],
                                                   prob[:, i % 2, q, k * P:(k + 1) * P], ident[:])
                last.then_inc(pT_mm, 1)

            def weigh(g, u, i):
                j, b = divmod(i, B)
                after(pe, pT_lo, u + 1)
                after(pe, v_lo, 8 * g + 2 * b + 2)
                after(pe, o_lo, u - 1)
                product(o_bank[i % 2][:, 0:S], lambda a, k: v[a][:, 2 * b + k, j * HD:(j + 1) * HD],
                        lambda a, k: pT[a][:, i % 2, k, :], range(QT)).then_inc(o_mm, 1)

            def project(g, t):
                after(pe, wo_lo, g + 1)
                after(pe, o_lo, 8 * g + B + t // 2 + 1)
                if isinstance(g, int) and g == NG - 1:
                    if t < 2:
                        pe.wait_ge(ffn_lo, 5)
                    else:
                        pe.wait_ge(last_gated, t - 1)
                elif t >= 2:
                    after(pe, attn_added, 8 * g + t - 1)
                else:
                    after(pe, v_lo, 8 * (g + 1) + 6 + t + 1)
                    pe.wait_ge(gate_ready, t + 1)
                product(aux_bank[t % 2][:, :], lambda a, j: oT[a][:, j, t * P:(t + 1) * P],
                        lambda a, j: wos[a][:, j, :], range(2)).then_inc(wo_mm, 1)

            def ffn_weights(n):
                ps = aux_bank[n % 2]
                if n < 2:
                    pe.wait_ge(attn_added, 8 * (NG - 2) + 6 + n + 1)
                else:
                    pe.wait_ge(ffn_lo, n - 1)
                if n == 0:
                    pe.wait_ge(lora_in, 16 * (1 + NR))
                    for i in range(KT):
                        last = nc.tensor.transpose(ps[:, i * P:(i + 1) * P], lora_b_raw[:, i * P:(i + 1) * P], ident[:])
                else:
                    cols = slice((n - 1) * P, n * P)
                    pe.wait_ge(ffn_lo, 1)
                    pe.wait_ge(lora_lo, 1)
                    for i, (a, b) in enumerate(PARTS):
                        mm(ps[:, :], lora_as[a][:, cols], bT[b], start=i == 0, stop=False)
                    pe.wait_ge(ffn_in, 32)
                    for i in range(KT):
                        last = mm(ps[:, i * P:(i + 1) * P], ffn_raw[i // 2][:, i % 2, cols], ident[:], start=False, stop=i == KT - 1)
                last.then_inc(ffn_mm, 1)

            def gate_rows():
                pe.wait_ge(gate_w_in, 32)
                for m in range(2):
                    pe.wait_ge(v_lo, 16 + m - 1)
                    for k in range(KT):
                        last = mm(aux_bank[m][0:B, :], cT[:, k, :], wmod_b[:, k, m * D:(m + 1) * D],
                                  start=k == 0, stop=k == KT - 1)
                    last.then_inc(gate_mm, 1)

            pe.wait_ge(rk_ready, 2)
            scores(0, 0, 0)
            scores(0, 1, 1)
            transposes(0, 0)
            scores(0, 2, 2)

            def pair_b(g):
                first, last = isinstance(g, int) and g == 0, isinstance(g, int) and g == NG - 1
                for i in range(UNITS):
                    u = UNITS * g + i
                    if not (last and i + 1 >= UNITS):
                        transposes(u + 1, (i + 1) % UNITS)
                    if not (last and i + 3 >= UNITS):
                        scores(g + (i + 3) // UNITS, u + 3, (i + 3) % UNITS)
                    if i < B and not first:
                        for t in (2 * i, 2 * i + 1):
                            project(g - 1, t)
                    if last:
                        for n in LAST_PAIR_BEFORE.get(i, ()):
                            ffn_weights(n)
                    if i < B and first:
                        if i == 0:
                            pe.wait_ge(mod_in, 32)
                            pe.wait_ge(v_lo, 8)
                        last_mm = mod_columns(aux_bank[0], wmod_b, (2 * i, 2 * i + 1))
                        if i == B - 1:
                            last_mm.then_inc(mod_mm, 1)
                    weigh(g, u, i)
                    if last:
                        for n in LAST_PAIR_AFTER.get(i, ()):
                            ffn_weights(n)
                    if i >= B and not last:
                        for s in (2 * (i - B), 2 * (i - B) + 1):
                            values(g + 1, s)
                    if first and i == UNITS - 1:
                        gate_rows()
                    if i > B and last:
                        for t in (2 * (i - B - 1), 2 * (i - B - 1) + 1):
                            project(g, t)

            loop_peeled(pe, NG, pair_b)

            def h2_transposes(b):
                pe.wait_ge(xn2, 2 * b + 2)
                for half in range(2):
                    n = 2 * b + half
                    after(pe, h2_affine, 2 * (n - 2) + 2)
                    for i in range(2):
                        for q in range(QT):
                            k = 2 * half + i
                            last = nc.tensor.transpose(bank[half][:, i * S + q * P:i * S + (q + 1) * P],
                                                       attn[:, 2 * b + q, k * P:(k + 1) * P], ident[:])
                    last.then_inc(h2_mm, 1)

            def ffn(b):
                for t in (2 * b, 2 * b + 1):
                    ps = bank[4 + t % 2]
                    after(pe, out_gated, t - 1)
                    pe.wait_ge(h2_lo, 2 * b + 2)
                    product(ps[:, :], lambda a, k: hT[a][:, k, t * P:(t + 1) * P], lambda a, k: ffnT[a][:, k, :],
                            range(KT)).then_inc(out_mm, 1)

            h2_transposes(0)
            for t in range(NT - 2, NT):
                project(NG - 1, t)
            for b in range(B):
                if b + 1 < B:
                    h2_transposes(b + 1)
                ffn(b)


_INS = ["L0_attn_hidden_states", "L0_attn_Wq", "L0_attn_bq", "L0_attn_Wk", "L0_attn_bk", "L0_attn_Wv", "L0_attn_bv",
        "L0_attn_Wo", "L0_attn_bo", "L0_attn_gq", "L0_attn_gk", "L0_ffn_lora_A", "L0_ffn_lora_B", "L0_ffn_W",
        "L0_ffn_bias", "L0_ffn_lora_weights", "L0_c", "L0_wmod"]


def kernel(**inputs):
    import numpy as np
    import concourse.bacc as bacc
    from concourse.bass_utils import run_bass_kernel_spmd

    nc = bacc.Bacc("TRN2", target_bir_lowering=False, num_devices=1)
    arrays, args = {}, []
    for name in _INS:
        a = np.ascontiguousarray(inputs[name])
        arrays[f"in_{name}"] = a
        args.append(nc.dram_tensor(f"in_{name}", a.shape, mybir.dt.from_np(a.dtype), kind="ExternalInput").ap())
    args.append(nc.dram_tensor("out_x", (B, S, D), F32, kind="ExternalOutput").ap())
    adaln_block(nc, *args)
    r = run_bass_kernel_spmd(nc, [arrays], core_ids=[0])
    return r.results[0]["out_x"]
```

```python
import concourse.bass as bass
from concourse import mybir
from concourse.alu_op_type import AluOpType as ALU
from contextlib import ExitStack


F32 = mybir.dt.float32
F32R = mybir.dt.float32r
ACT = mybir.ActivationFunctionType
AX = mybir.AxisListType

B, S, D = 4, 256, 512
H, HD = 32, 128
INNER = H * HD
T = B * S
P = 128
KT = D // P
NT = T // P
QT = S // P
HALF = T // 2
NG = H // 2
UNITS = 2 * B
NU = NG * UNITS
LN_EPS, RMS_EPS = 1e-5, 1e-6
SOFTMAX_SCALE = HD ** -0.5
NR, RANK = 8, 16
LORA_SCALE = 2.0
X_BANK = (1, 3, 5, 7) * 2
PARTS = ((0, 0), (0, 1), (1, 0))
SA, CA, GA, SB, CB, GB = range(6)


LAST_PAIR_BEFORE = {4: (1, 2)}
LAST_PAIR_AFTER = {3: (0,), 4: (3, 4)}


def after(eng, sem, n):
    if isinstance(n, int) and n <= 0:
        return
    eng.wait_ge(sem, n)


def loop_peeled(eng, n, body):
    body(0)
    with eng.Fori(1, n - 1) as i:
        body(i)
    body(n - 1)


def adaln_block(nc, x, wq, bq, wk, bk, wv, bv, wo, bo, gq, gk, lora_a, lora_b, w_ffn, b_ffn,
                lora_w, c, wmod, out):
    ctx = ExitStack()
    with ctx:
        def sb(name, shape, dt=F32):
            return ctx.enter_context(nc.sbuf_tensor(name, shape, dt))

        def sem(name):
            return ctx.enter_context(nc.semaphore(name))

        qk_dram = nc.dram_tensor("qk_spill", [H, 2, P, T], F32, kind="Internal").ap()
        gate_dram = nc.dram_tensor("gate_rows", [2, B, D], F32, kind="Internal").ap()

        hT = [sb("hT_hi", [P, KT, T], F32R), sb("hT_lo", [P, KT, T], F32R)]
        attn = sb("attn", [P, NT, D])
        v = [sb("v_hi", [P, NT, 2 * HD], F32R), sb("v_lo", [P, NT, 2 * HD], F32R)]
        wv_raw = sb("wv_raw", [P, KT, 2 * HD])
        wvs = [sb("wv_hi", [P, KT, 2 * HD], F32R), sb("wv_lo", [P, KT, 2 * HD], F32R)]
        wo_raw = sb("wo_raw", [P, 2, D])
        wos = [sb("wo_hi", [P, 2, D], F32R), sb("wo_lo", [P, 2, D], F32R)]
        qk_raw = sb("qk_raw", [P, 2, 2, T])
        qks = [sb("qk_hi", [P, 2, 2, T], F32R), sb("qk_lo", [P, 2, 2, T], F32R)]
        prob = sb("prob", [P, 2, QT, S])
        pT = [sb("pT_hi", [P, 2, QT, S], F32R), sb("pT_lo", [P, 2, QT, S], F32R)]
        oT = [sb("oT_hi", [P, 2, T], F32R), sb("oT_lo", [P, 2, T], F32R)]
        rk = sb("rk", [P, T])
        wstage = sb("wstage", [P, 4096])
        ident = sb("ident", [P, P])
        ones = sb("ones", [P, P])
        vec_rows = sb("vec_rows", [H, 5, HD])
        vec = sb("vec", [P, 5, H])
        vec_now = sb("vec_now", [P, 2, 5])
        c_row = sb("c_row", [B, D])
        silu = sb("silu", [P, 4, KT * B])
        cT = sb("cT", [P, KT, B])
        mod1 = sb("mod1", [P, 2, KT, B])
        mod2 = sb("mod2", [P, 2, KT, B])
        stats = sb("stats", [P, NT, 6])
        mv = sb("mv", [P, NT, 2])
        norm = sb("norm", [P, 4, NT])
        rms = sb("rms", [P, 4, 2 * NT])
        qscale = sb("qscale", [P, 2, NT])
        rowmax = sb("rowmax", [P, 2, QT])
        negmax = sb("negmax", [P, 2, QT])
        rowsum = sb("rowsum", [P, 2, QT])
        rowinv = sb("rowinv", [P, 2, QT])
        exp_table = sb("exp_table", [P, 1])
        lora_coef = sb("lora_coef", [P, 2])
        gate_row = sb("gate_row", [B, 2, D])
        gate_sign = sb("gate_sign", [B, 2, D])
        mod_row = gate_sign[:, :, :]

        w_raw = wstage[:, 0:2048].rearrange("p (j w k n) -> p j w k n", j=2, w=2, k=KT)
        ws = [t[:, :, :, 0:D].rearrange("p j w (k n) -> p j w k n", k=KT) for t in qks]
        square = attn[:, 0:4, :]
        sumsq = attn[:, 4:8, :]
        x_sb = qk_raw[:, :, :, :].rearrange("p j w t -> p (j w t)").rearrange("p (n d) -> p n d", n=NT)
        wmod_a = attn[:, :, :].rearrange("p n d -> p (n d)").rearrange("p (k m) -> p k m", k=KT)
        wmod_b = wstage[:, :].rearrange("p (k m) -> p k m", k=KT)
        h_tmp = [prob[:, n, :, :].rearrange("p q s -> p (q s)") for n in range(2)] + [
            rk[:, n * HALF:(n + 1) * HALF] for n in range(2)]
        ffn_raw = [t.rearrange("p (o d) -> p o d", o=2) for t in (
            wv_raw[:, :, :].rearrange("p k n -> p (k n)"), rk[:, :])]
        lora_a_raw, lora_b_raw = x_sb[:, 6, :], x_sb[:, 7, :]
        ffnT = [t[:, 0, :, :].rearrange("p w t -> p (w t)").rearrange("p (k o) -> p k o", k=KT) for t in qks]
        lora_as = [t[:, :, :].rearrange("p k n -> p (k n)")[:, 0:D] for t in wvs]
        bT = [t[:, :, :].rearrange("p k n -> p (k n)")[:, D:2 * D] for t in wvs]
        gates = wstage[:, :].rearrange("p (g b d) -> p g b d", g=2, b=B)
        bias_bc = wo_raw[:, 0, :]
        h2_tmp = prob[:, :, :, :].rearrange("p a q s -> p a (q s)")
        gb_bias = wv_raw[:, :, :].rearrange("p k n -> p (k n)").rearrange("p (a d) -> p a d", a=2)

        bank = [ctx.enter_context(nc.psum_tensor(f"bank{i}", [P, 512], F32)) for i in range(8)]
        s_bank = [bank[0], bank[1]]
        pT_bank = [bank[2], bank[3]]
        o_bank = [bank[4], bank[5]]
        aux_bank = [bank[6], bank[7]]
        last_bank = aux_bank * 2 + pT_bank + aux_bank
        first_v_bank = [bank[0], bank[1]] + aux_bank * 3

        x_in = [sem(f"x_in{i}") for i in range(NT // 2)]
        small_in, mod1_in, mod2_in = sem("small_in"), [sem(f"mod1_in{k}") for k in range(KT)], sem("mod2_in")
        ident_ready, ones_ready = sem("ident_ready"), sem("ones_ready")
        dve_step = sem("dve_step")
        stat_ready, root_ready = sem("stat_ready"), sem("root_ready")
        c_in, c_exp, cT_mm, cT_ready = sem("c_in"), sem("c_exp"), sem("cT_mm"), sem("cT_ready")
        vec_mm, vec_ready = sem("vec_mm"), sem("vec_ready")
        coef_ready = sem("coef_ready")
        vec_now_a, vec_now_b = sem("vec_now_a"), sem("vec_now_b")
        mod_row_mm, mod_row_ready = sem("mod_row_mm"), sem("mod_row_ready")
        mod_mm, mod_ready = sem("mod_mm"), sem("mod_ready")
        xn_ready, hT_mm, h_affine, hT_hi_ready, hT_lo_ready = (
            sem("xn_ready"), sem("hT_mm"), sem("h_affine"), sem("hT_hi_ready"), sem("hT_lo_ready"))
        w_in = [sem("w_in0"), sem("w_in1")]
        w_hi, w_lo = sem("w_hi"), sem("w_lo")
        proj_mm, squared, summed, scaled = sem("proj_mm"), sem("squared"), sem("summed"), sem("scaled")
        spilled = [sem("spilled0"), sem("spilled1")]
        rms_mm, rms_var, rms_root, rms_cols = sem("rms_mm"), sem("rms_var"), sem("rms_root"), sem("rms_cols")
        rk_mm, rk_ready = sem("rk_mm"), sem("rk_ready")
        wv_in, wo_in, bo_in = sem("wv_in"), sem("wo_in"), sem("bo_in")
        wv_hi, wv_lo, wo_hi, wo_lo = sem("wv_hi_done"), sem("wv_lo_done"), sem("wo_hi_done"), sem("wo_lo_done")
        qk_in = [sem("qk_in0"), sem("qk_in1")]
        k_normed, qk_hi, qk_lo = sem("k_normed"), sem("qk_hi_done"), sem("qk_lo_done")
        score_mm, max_done, negmax_done, exp_done, inv_done, prob_ready = (
            sem("score_mm"), sem("max_done"), sem("negmax_done"), sem("exp_done"), sem("inv_done"), sem("prob_ready"))
        pT_mm, pT_hi, pT_lo = sem("pT_mm"), sem("pT_hi_done"), sem("pT_lo_done")
        o_mm, o_hi, o_lo = sem("o_mm"), sem("o_hi_done"), sem("o_lo_done")
        v_mm, v_hi, v_lo = sem("v_mm"), sem("v_hi_done"), sem("v_lo_done")
        wo_mm, attn_added = sem("wo_mm"), sem("attn_added")
        ffn_in, ffn_mm, ffn_hi, ffn_lo = sem("ffn_in"), sem("ffn_mm"), sem("ffn_hi"), sem("ffn_lo")
        gate_stored, gate_in, bias_in, x_again = (
            sem("gate_stored"), sem("gate_in"), sem("bias_in"), [sem(f"x_again{i}") for i in range(B)])
        gate_mm, lora_in = sem("gate_mm"), sem("lora_in")
        gate_ready, gate_w_in = sem("gate_ready"), sem("gate_w_in")
        attn_gated, x_under, last_gated, x_done, last_x_done = sem("attn_gated"), sem("x_under"), sem("last_gated"), sem("x_done"), sem("last_x_done")
        norm2_ready, var2, root2, xn2, h2_mm, h2_affine, h2_hi, h2_lo = (
            sem("norm2_ready"), sem("var2"), sem("root2"), sem("xn2"), sem("h2_mm"), sem("h2_affine"), sem("h2_hi"), sem("h2_lo"))
        lora_hi, lora_lo = sem("lora_hi"), sem("lora_lo")
        bias_gated, x_biased, out_ready_last, out_mm, out_gated, out_ready, stored = (
            sem("bias_gated"), sem("x_biased"), sem("out_ready_last"), sem("out_mm"), sem("out_gated"), sem("out_ready"), sem("stored"))

        x_tiles = x.rearrange("b (q p) d -> p (b q) d", p=P)
        out_tiles = out.rearrange("b (q p) d -> p (b q) d", p=P)
        wmod_t = wmod.rearrange("(k p) m -> p k m", p=P)
        w_t = [w.rearrange("(k p) (h n) -> h p k n", p=P, n=HD) for w in (wq, wk)]
        wv_t = wv.rearrange("(k p) (g n) -> g p k n", p=P, n=2 * HD)
        wo_t = wo.rearrange("(g j p) n -> g p j n", p=P, j=2)

        def at(ap, i):
            if isinstance(i, int):
                return ap[i]
            return ap[bass.ds(i, 1)].rearrange("o ... -> (o ...)") if len(ap.shape) == 1 else drop(ap[bass.ds(i, 1)])

        def drop(ap):
            names = "abcdefg"[:len(ap.shape) - 1]
            return ap.rearrange(f"o {' '.join(names)} -> (o {names[0]}) {' '.join(names[1:])}")

        block = ctx.enter_context(nc.Block())

        @block.sync
        def _(sp):
            def first_x(t):
                sp.dma_start(x_sb[:, t:t + 2, :], x_tiles[:, t:t + 2, :]).then_inc(x_in[t // 2], 16)

            first_x(0)
            first_x(2)
            for k in range(KT):
                sp.dma_start(wmod_a[:, k, :], wmod_t[:, k, 0:2 * D]).then_inc(mod1_in[k], 16)

            def load_w(h, j):
                for w in range(2):
                    sp.dma_start(w_raw[:, j, w], at(w_t[w], h)).then_inc(w_in[j], 16)

            for j in range(2):
                load_w(j, j)
            first_x(4)
            first_x(6)

            def load_qk(g, j):
                for w in (1, 0):
                    sp.dma_start(qk_raw[:, j, w, :], at(qk_dram, 2 * g + j)[w]).then_inc(qk_in[j], 16)

            def pair_a(g):
                for j in range(2):
                    h = 2 * g + j
                    if not (isinstance(g, int) and g == NG - 1):
                        after(sp, w_lo, 2 * h + 2)
                        load_w(h + 2, j)
                    if isinstance(g, int) and h == H - 1:
                        after(sp, spilled[0], 32 * NG)
                        load_qk(0, 0)
                    for w in range(2):
                        after(sp, scaled, 4 * h + 2 * w + 2)
                        sp.dma_start(at(qk_dram, h)[w], qk_raw[:, j, w, :]).then_inc(spilled[j], 16)

            loop_peeled(sp, NG, pair_a)

            after(sp, spilled[1], 32 * NG)
            load_qk(0, 1)
            after(sp, w_lo, 2 * H)
            sp.dma_start(wmod_b[:, :, :], wmod_t[:, :, SB * D:(CB + 1) * D]).then_inc(mod2_in, 16)
            after(sp, rms_mm, 1)
            sp.dma_start(attn[:, :, :], bo.rearrange("(a b d) -> a b d", a=1, b=1).to_broadcast([P, NT, D])).then_inc(bo_in, 16)

            def pair_b(g):
                last = isinstance(g, int) and g == NG - 1
                if not last:
                    for j in range(2):
                        after(sp, qk_lo, 2 * (2 * g + j) + 2)
                        load_qk(g + 1, j)
                if isinstance(g, int) and g == 0:
                    after(sp, mod_row_mm, 3)
                    for i, m in enumerate((GA, GB)):
                        sp.dma_start(wmod_b[:, :, i * D:(i + 1) * D], wmod_t[:, :, m * D:(m + 1) * D]).then_inc(gate_w_in, 16)
                if last:
                    after(sp, gate_ready, 2)
                    sp.dma_start(gate_dram.rearrange("g b d -> b g d"), gate_row[:, :, :]).then_inc(gate_stored, 16)
                    sp.wait_ge(gate_stored, 16)
                    for m in range(2):
                        sp.dma_start(gates[:, m], gate_dram[m].rearrange("(a b) d -> a b d", a=1).to_broadcast([P, B, D])).then_inc(gate_in, 16)

            loop_peeled(sp, NG, pair_b)

            ffn_tiles = w_ffn.rearrange("(a o p) d -> a p o d", p=P, o=2)
            after(sp, wv_lo, NG)
            sp.dma_start(ffn_raw[0], ffn_tiles[0]).then_inc(ffn_in, 16)

            def load_x(t):
                sp.dma_start(x_sb[:, t:t + 2, :], x_tiles[:, t:t + 2, :]).then_inc(x_again[t // 2], 16)

            after(sp, qk_lo, 2 * (H - 1))
            load_x(0)
            load_x(2)
            after(sp, qk_lo, 2 * H)
            sp.dma_start(lora_a_raw, lora_a.rearrange("n r d -> (n r) d")).then_inc(lora_in, 16)
            for n in range(NR):
                sp.dma_start(lora_b_raw.rearrange("p (o n r) -> p o n r", n=NR, r=RANK)[:, :, n, :],
                             lora_b[n].rearrange("(o p) r -> p o r", p=P)).then_inc(lora_in, 16)
            load_x(4)
            sp.dma_start(ffn_raw[1], ffn_tiles[1]).then_inc(ffn_in, 16)
            after(sp, lora_lo, 1)
            after(sp, ffn_mm, 1)
            load_x(6)
            after(sp, wo_lo, NG)
            sp.dma_start(bias_bc, b_ffn.rearrange("(a d) -> a d", a=1).to_broadcast([P, D])).then_inc(bias_in, 16)
            for t in range(NT):
                if t < 6:
                    after(sp, out_ready, t + 1)
                else:
                    after(sp, out_ready_last, t - 5)
                sp.dma_start(out_tiles[:, t, :], attn[:, t, :]).then_inc(stored, 16)
            sp.wait_ge(stored, 16 * NT)

        @block.gpsimd
        def _(pool):
            nc.gpsimd.memset(ones[:], 1.0).then_inc(ones_ready, 1)
            nc.gpsimd.memset(ident[:], 0.0).then_inc(ident_ready, 1)
            pool.wait_ge(ident_ready, 1)
            nc.gpsimd.affine_select(out=ident[:], in_=ident[:], compare_op=ALU.not_equal, fill=1.0, base=0,
                                    pattern=[[-1, P]], channel_multiplier=1).then_inc(ident_ready, 1)
            pool.dma_start(wv_raw[:, :, :], wv_t[0]).then_inc(wv_in, 16)
            pool.dma_start(wo_raw[:, :, :], wo_t[0]).then_inc(wo_in, 16)

            def pair_a(g):
                for j in range(2):
                    h = 2 * g + j
                    for s in range(4):
                        after(pool, squared, 4 * h + s + 1)
                        after(pool, summed, 4 * h - 4 + s + 1)
                        if isinstance(g, int) and h == 0:
                            nc.gpsimd.tensor_copy(sumsq[:, s], square[:, s]).then_inc(summed, 1)
                        else:
                            nc.gpsimd.tensor_tensor(sumsq[:, s], sumsq[:, s], square[:, s], ALU.add).then_inc(summed, 1)

            def split_lo(dst, raw, hi, done):
                nc.gpsimd.tensor_tensor(dst, raw, hi.bitcast(F32), ALU.subtract).then_inc(done, 1)

            def norm_k(g, j):
                after(pool, qk_in[j], 32 * (g + 1))
                nc.gpsimd.tensor_tensor(qk_raw[:, j, 1, :], qk_raw[:, j, 1, :], rk[:, :], ALU.mult).then_inc(k_normed, 1)

            def lo_qk(g, j, parts=(0, 1)):
                for w in parts:
                    after(pool, qk_hi, 2 * (2 * g + j) + w + 1)
                    split_lo(qks[1][:, j, w, :], qk_raw[:, j, w, :], qks[0][:, j, w, :], qk_lo)

            def lo_wv(g):
                after(pool, wv_hi, g + 1)
                split_lo(wvs[1][:, :, :], wv_raw[:, :, :], wvs[0][:, :, :], wv_lo)

            def lo_wo(g):
                after(pool, wo_hi, g + 1)
                split_lo(wos[1][:, :, :], wo_raw[:, :, :], wos[0][:, :, :], wo_lo)

            for j in range(2):
                for w in range(2):
                    pool.wait_ge(w_hi, 2 * j + w + 1)
                    split_lo(ws[1][:, j, w], w_raw[:, j, w], ws[0][:, j, w], w_lo)
            lo_wv(0)
            pool.wait_ge(wv_lo, 1)
            pool.dma_start(wv_raw[:, :, :], wv_t[1]).then_inc(wv_in, 16)
            loop_peeled(pool, NG, pair_a)
            lo_qk(0, 0, (0,))
            pool.wait_ge(k_normed, 1)
            norm_k(0, 1)
            pool.wait_ge(qk_lo, 2)
            lo_qk(0, 1)

            def pair_b(g):
                last = isinstance(g, int) and g == NG - 1
                if not last:
                    if not (isinstance(g, int) and g == 0):
                        after(pool, wv_lo, g + 1)
                        pool.dma_start(wv_raw[:, :, :], at(wv_t, g + 1)).then_inc(wv_in, 16)
                    norm_k(g + 1, 0)
                    lo_wv(g + 1)
                    lo_qk(g + 1, 0)
                if last:
                    pool.wait_ge(lora_hi, 1)
                    split_lo(lora_as[1], lora_a_raw, lora_as[0], lora_lo)
                    pool.wait_ge(gate_in, 32)
                    for t in range(6):
                        x_and_attn(t)
                lo_wo(g)
                if not last:
                    after(pool, wo_lo, g + 1)
                    pool.dma_start(wo_raw[:, :, :], at(wo_t, g + 1)).then_inc(wo_in, 16)
                    norm_k(g + 1, 1)
                    lo_qk(g + 1, 1)

            def x_and_attn(t):
                pool.wait_ge(attn_added, 8 * (NG - 2) + t + 1)
                nc.gpsimd.tensor_tensor(attn[:, t], attn[:, t], gates[:, 0, t // QT], ALU.mult).then_inc(attn_gated, 1)
                pool.wait_ge(attn_gated, t + 1)
                pool.wait_ge(x_again[t // 2], 16)
                nc.gpsimd.tensor_tensor(attn[:, t], attn[:, t], x_sb[:, t, :], ALU.add).then_inc(x_under, 1)

            loop_peeled(pool, NG, pair_b)

            for t in range(6, NT):
                x_and_attn(t)
            def add_last(b):
                for t in (2 * b, 2 * b + 1):
                    pool.wait_ge(last_gated, t + 1)
                    nc.gpsimd.tensor_tensor(x_sb[:, t], x_sb[:, t], attn[:, t], ALU.add).then_inc(x_done, 1)

            for b in range(B - 1):
                add_last(b)
            pool.wait_ge(bias_in, 16)
            pool.wait_ge(ffn_mm, 5)
            for b in range(B):
                after(pool, x_biased, 2 * b - 2)
                nc.gpsimd.tensor_tensor(gb_bias[:, b % 2], gates[:, 1, b], bias_bc, ALU.mult).then_inc(bias_gated, 1)
                pool.wait_ge(bias_gated, b + 1)
                for t in (2 * b, 2 * b + 1):
                    pool.wait_ge(xn2, t + 1)
                    nc.gpsimd.tensor_tensor(x_sb[:, t], x_sb[:, t], gb_bias[:, b % 2], ALU.add).then_inc(x_biased, 1)
                if b >= 1:
                    for t in (2 * b - 2, 2 * b - 1):
                        pool.wait_ge(x_biased, t + 1)
                        pool.wait_ge(out_gated, t + 1)
                        nc.gpsimd.tensor_tensor(attn[:, t], attn[:, t], x_sb[:, t], ALU.add).then_inc(out_ready, 1)

        @block.scalar
        def _(act):
            act.dma_start(c_row[:, :], c).then_inc(c_in, 16)
            for i, a in enumerate((bq, bk, gq, gk, bv)):
                act.dma_start(vec_rows[:, i, :], a.rearrange("(h n) -> h n", n=HD)).then_inc(small_in, 16)
            lw = lora_w.rearrange("(n a b) -> n a b", a=1, b=1)
            act.dma_start(lora_coef[:, 0:1], lw.to_broadcast([NR, RANK, 1])).then_inc(small_in, 16)

            act.wait_ge(cT_mm, 1)
            nc.scalar.activation(silu[:, 1, :], bank[0][:, 0:KT * B], ACT.Exp, scale=-1.0).then_inc(c_exp, 1)
            def first_root(half):
                four = slice(4 * half, 4 * half + 4)
                act.wait_ge(stat_ready, half + 1)
                nc.scalar.activation(norm[:, 1, four], norm[:, 0, four], ACT.Sqrt).then_inc(root_ready, 1)

            first_root(0)

            def copy_mod_row(n, ps):
                act.wait_ge(mod_row_mm, max(n, 1))
                nc.scalar.activation(mod_row[:, n % 2, :], ps[0:B, :], ACT.Copy).then_inc(mod_row_ready, 1)

            copy_mod_row(0, bank[4])

            def first_w_hi(j):
                act.wait_ge(w_in[j], 32)
                for w in range(2):
                    nc.scalar.activation(ws[0][:, j, w], w_raw[:, j, w], ACT.Copy).then_inc(w_hi, 1)

            first_w_hi(0)

            for n in range(2 * KT):
                half, k = divmod(n, KT)
                if n == KT:
                    first_w_hi(1)
                    first_root(1)
                act.wait_ge(hT_mm, n + 1)
                if n == 0:
                    act.wait_ge(mod_ready, 2)
                if n >= 4:
                    act.wait_ge(hT_lo_ready, n - 3)
                for i in range(2):
                    b = 2 * half + i
                    nc.scalar.activation(h_tmp[n % 4][:, i * S:(i + 1) * S], bank[X_BANK[n]][:, i * S:(i + 1) * S], ACT.Identity,
                                         scale=mod1[:, 1, k, b:b + 1], bias=mod1[:, 0, k, b:b + 1]).then_inc(h_affine, 1)

            def pair_a(g):
                for j in range(2):
                    h = 2 * g + j
                    for s in range(4):
                        w = s // 2
                        if isinstance(g, int) and g == 0:
                            act.wait_ge(proj_mm, (6, 8)[j])
                        else:
                            after(act, proj_mm, 4 * h + s + 1)
                        after(act, summed, 4 * h - 4 + s + 1)
                        if s == 0:
                            after(act, vec_now_a, h + 1)
                        nc.scalar.activation(square[:, s], bank[4 * j + s][:, :], ACT.Square,
                                             bias=vec_now[:, j, w:w + 1]).then_inc(squared, 1)

            def hi_copy(dst, src, done):
                nc.scalar.activation(dst, src, ACT.Copy).then_inc(done, 1)

            def hi_wv(g):
                after(act, wv_in, 16 * (g + 1))
                after(act, v_mm, 8 * g)
                hi_copy(wvs[0][:, :, :], wv_raw[:, :, :], wv_hi)

            def hi_wo(g):
                after(act, wo_in, 16 * (g + 1))
                after(act, wo_mm, 8 * g)
                hi_copy(wos[0][:, :, :], wo_raw[:, :, :], wo_hi)

            def hi_qk(g, j, w):
                h = 2 * g + j
                if w:
                    after(act, k_normed, h + 1)
                else:
                    after(act, qk_in[j], 32 * (g + 1))
                after(act, score_mm, 4 * (h - 1))
                if isinstance(g, int) and g == 0:
                    act.wait_ge(proj_mm, 4 * (H - 1 + j))
                hi_copy(qks[0][:, j, w, :], qk_raw[:, j, w, :], qk_hi)

            def hi_v(n, s):
                after(act, v_mm, n + 1)
                ps = first_v_bank[s] if isinstance(n, int) and n < NT else aux_bank[s % 2]
                hi_copy(v[0][:, s, :], ps[:, 0:2 * HD], v_hi)

            def exp(g, u, i):
                b = i % B
                after(act, negmax_done, u + 1)
                after(act, pT_mm, u - 1)
                for q in range(QT):
                    t = QT * b + q
                    nc.scalar.activation(prob[:, i % 2, q, :], s_bank[i % 2][:, q * S:(q + 1) * S], ACT.Exp,
                                         scale=qscale[:, 0, t:t + 1], bias=negmax[:, i % 2, q:q + 1],
                                         accum_out=rowsum[:, i % 2, q:q + 1]).then_inc(exp_done, 1)

            def hi_pT(u, i):
                after(act, pT_mm, u + 1)
                after(act, o_mm, u - 1)
                hi_copy(pT[0][:, i % 2, :, :], pT_bank[i % 2][:, :].rearrange("p (k q) -> p k q", k=QT), pT_hi)

            def hi_o(u, i, h):
                j, b = divmod(i, B)
                after(act, o_mm, u + 1)
                if b == 0:
                    after(act, vec_now_b, h + 1)
                nc.scalar.activation(oT[0][:, j, b * S:(b + 1) * S], o_bank[i % 2][:, 0:S], ACT.Identity,
                                     bias=vec_now[:, j, 4:5]).then_inc(o_hi, 1)

            def root(b):
                act.wait_ge(var2, b + 1)
                nc.scalar.activation(norm[:, 1, 2 * b:2 * b + 2], norm[:, 0, 2 * b:2 * b + 2], ACT.Sqrt).then_inc(root2, 1)

            def apply_norm(b):
                act.wait_ge(norm2_ready, b + 1)
                for t in (2 * b, 2 * b + 1):
                    nc.scalar.activation(attn[:, t, :], x_sb[:, t, :], ACT.Identity, scale=norm[:, 2, t:t + 1],
                                         bias=norm[:, 3, t:t + 1]).then_inc(xn2, 1)

            hi_wv(0)
            loop_peeled(act, NG, pair_a)

            hi_qk(0, 0, 0)
            for s in range(2):
                hi_v(s, s)
            act.wait_ge(rms_var, 1)
            nc.scalar.activation(rms[:, 1, :], rms[:, 0, :], ACT.Sqrt).then_inc(rms_root, 1)
            nc.scalar.activation(exp_table[:, :], ones[:, 0:1], ACT.Exp)
            hi_v(2, 2)
            act.wait_ge(rk_mm, 1)
            nc.scalar.activation(rk[:, HALF:T], bank[1][:, :], ACT.Copy).then_inc(rk_ready, 1)
            hi_v(3, 3)
            hi_qk(0, 0, 1)
            hi_v(4, 4)
            hi_v(5, 5)
            exp(0, 0, 0)
            exp(0, 1, 1)
            hi_qk(0, 1, 0)
            hi_v(6, 6)
            hi_pT(0, 0)
            hi_qk(0, 1, 1)
            exp(0, 2, 2)

            def pair_b(g):
                first, last = isinstance(g, int) and g == 0, isinstance(g, int) and g == NG - 1
                for i in range(UNITS):
                    u = UNITS * g + i
                    if not (last and i + 1 >= UNITS):
                        hi_pT(u + 1, (i + 1) % UNITS)
                    if first and i == 0:
                        hi_v(7, 7)
                    if i == 0 and not last:
                        hi_wv(g + 1)
                    if i in (1, 2) and not last:
                        hi_qk(g + 1, 0, i - 1)
                    if i == 4:
                        hi_wo(g)
                    if i in (5, 6) and not last:
                        hi_qk(g + 1, 1, i - 5)
                    if not (last and i + 3 >= UNITS):
                        exp(g, u + 3, (i + 3) % UNITS)
                    if last:
                        for n in LAST_PAIR_BEFORE.get(i, ()):
                            hi_ffn(n)
                    hi_o(u, i, 2 * g + i // B)
                    if first and i in (1, 2):
                        copy_mod_row(1 + i, aux_bank[i - 1])
                    if i >= B and not last:
                        for t in range(2):
                            s = 2 * (i - B) + t
                            hi_v(8 * (g + 1) + s, s)
                    if last:
                        if i == 0:
                            act.wait_ge(lora_in, 16 * (1 + NR))
                            act.wait_ge(v_mm, 8 * NG)
                            hi_copy(lora_as[0], lora_a_raw, lora_hi)
                        for n in LAST_PAIR_AFTER.get(i, ()):
                            hi_ffn(n)
                        if i == UNITS - 1:
                            apply_norm(0)
                        if i > B + 1:
                            root(i - B - 2)

            def hi_ffn(n):
                act.wait_ge(ffn_mm, n + 1)
                if n == 0:
                    act.wait_ge(coef_ready, 1)
                    nc.scalar.activation(bT[0], aux_bank[0][:, :], ACT.Copy, scale=lora_coef[:, 1:2]).then_inc(ffn_hi, 1)
                else:
                    hi_copy(ffnT[0][:, n - 1, :], aux_bank[n % 2][:, :], ffn_hi)

            loop_peeled(act, NG, pair_b)

            def affine(b):
                for half in range(2):
                    n = 2 * b + half
                    act.wait_ge(h2_mm, n + 1)
                    after(act, h2_lo, n - 1)
                    for i in range(2):
                        k = 2 * half + i
                        nc.scalar.activation(h2_tmp[:, n % 2, i * S:(i + 1) * S], bank[half][:, i * S:(i + 1) * S],
                                             ACT.Identity, scale=mod2[:, 1, k, b:b + 1],
                                             bias=mod2[:, 0, k, b:b + 1]).then_inc(h2_affine, 1)
                    act.wait_ge(h2_affine, 2 * n + 2)
                    nc.scalar.activation(hT[0][:, 2 * half:2 * half + 2, b * S:(b + 1) * S],
                                         h2_tmp[:, n % 2, :].rearrange("p (k t) -> p k t", k=2), ACT.Copy).then_inc(h2_hi, 1)

            affine(0)
            root(2)
            apply_norm(1)
            affine(1)
            apply_norm(2)
            root(3)
            apply_norm(3)
            affine(2)
            affine(3)

        @block.vector
        def _(dve):
            steps = [0]

            def link(ins):
                steps[0] += 1
                ins.then_inc(dve_step, 1)
                dve.wait_ge(dve_step, steps[0])

            def newton(y, var, tmp):
                link(nc.vector.tensor_tensor(tmp, y, y, ALU.mult))
                link(nc.vector.tensor_tensor(tmp, tmp, var, ALU.mult))
                link(nc.vector.tensor_scalar(tmp, tmp, -0.5, 1.5, ALU.mult, ALU.add))
                return nc.vector.tensor_tensor(y, y, tmp, ALU.mult)

            dve.wait_ge(c_exp, 1)
            link(nc.vector.tensor_copy(silu[:, 0, :], bank[0][:, 0:KT * B]))
            link(nc.vector.tensor_scalar(silu[:, 2, :], silu[:, 1, :], 1.0, None, ALU.add))
            link(nc.vector.reciprocal(silu[:, 3, :], silu[:, 2, :]))
            nc.vector.tensor_tensor(cT[:, :, :].rearrange("p k b -> p (k b)"), silu[:, 0, :], silu[:, 3, :],
                                    ALU.mult).then_inc(cT_ready, 1)
            def modulation(dst, ps, n):
                cols = ps[:, 0:2 * KT * B].rearrange("p (m k b) -> p m k b", m=2, k=KT)
                dve.wait_ge(mod_mm, n + 1)
                nc.vector.tensor_copy(dst[:, 0], cols[:, 0]).then_inc(mod_ready, 1)
                nc.vector.tensor_scalar(dst[:, 1], cols[:, 1], 1.0, None, ALU.add).then_inc(mod_ready, 1)

            def start_norm(half):
                four = slice(4 * half, 4 * half + 4)
                for t in range(4 * half, 4 * half + 4):
                    if t % 2 == 0:
                        dve.wait_ge(x_in[t // 2], 16)
                    last = nc.vector.bn_stats(stats[:, t, :], x_sb[:, t, :])
                link(last)
                for t in range(4 * half, 4 * half + 4):
                    last = nc.vector.bn_aggr(mv[:, t, :], stats[:, t, :])
                link(last)
                nc.vector.tensor_scalar(norm[:, 0, four], mv[:, four, 1], LN_EPS, None, ALU.add).then_inc(stat_ready, 1)
                dve.wait_ge(root_ready, half + 1)
                link(nc.vector.reciprocal(norm[:, 2, four], norm[:, 1, four]))
                link(newton(norm[:, 2, four], norm[:, 0, four], norm[:, 3, four]))
                for t in range(4 * half, 4 * half + 4):
                    nc.vector.tensor_scalar(x_sb[:, t, :], x_sb[:, t, :], mv[:, t, 0:1], norm[:, 2, t:t + 1],
                                            ALU.subtract, ALU.mult).then_inc(xn_ready, 1)

            start_norm(0)

            def split_w(g, j):
                h = 2 * g + j
                after(dve, w_in[j], 32 * (g + 1))
                after(dve, proj_mm, 6 if isinstance(h, int) and h == 2 else 4 * (h - 1))
                for w in range(2):
                    nc.vector.tensor_copy(ws[0][:, j, w], w_raw[:, j, w]).then_inc(w_hi, 1)
                for w in range(2):
                    after(dve, w_hi, 2 * h + w + 1)
                    nc.vector.tensor_tensor(ws[1][:, j, w], w_raw[:, j, w], ws[0][:, j, w].bitcast(F32),
                                            ALU.subtract).then_inc(w_lo, 1)

            def take_vectors(h, j, done):
                src = vec[:, :, h:h + 1] if isinstance(h, int) else vec[:, :, bass.ds(h, 1)]
                nc.vector.tensor_scalar(vec_now[:, j, :], src.rearrange("p a o -> p (a o)"), 1.0, None, ALU.mult).then_inc(done, 1)


            dve.wait_ge(small_in, 96)
            nc.vector.tensor_scalar(lora_coef[:, 1:2], lora_coef[:, 0:1], LORA_SCALE, None, ALU.mult).then_inc(coef_ready, 1)
            dve.wait_ge(mod_row_mm, 1)
            nc.vector.tensor_copy(mod_row[:, 1, :], bank[6][0:B, :]).then_inc(mod_row_ready, 1)
            dve.wait_ge(vec_mm, 1)
            nc.vector.tensor_copy(vec[:, :, :], bank[2][:, 0:5 * H].rearrange("p (a h) -> p a h", a=5)).then_inc(vec_ready, 1)
            modulation(mod1, bank[2][:, 5 * H:], 0)
            dve.wait_ge(vec_ready, 1)

            for n in range(2 * KT):
                half, k = divmod(n, KT)
                if n == KT:
                    start_norm(1)
                dve.wait_ge(h_affine, 2 * n + 2)
                hi = hT[0][:, k, half * HALF:(half + 1) * HALF]
                nc.vector.tensor_copy(hi, h_tmp[n % 4]).then_inc(hT_hi_ready, 1)
                dve.wait_ge(hT_hi_ready, n + 1)
                nc.vector.tensor_tensor(hT[1][:, k, half * HALF:(half + 1) * HALF], h_tmp[n % 4], hi.bitcast(F32),
                                        ALU.subtract).then_inc(hT_lo_ready, 1)

            def pair_a(g):
                for j in range(2):
                    h = 2 * g + j
                    if isinstance(g, int) and g == 0:
                        if j == 0:
                            dve.wait_ge(w_lo, 4)
                            split_w(1, 0)
                    elif j == 0:
                        split_w(g, 1)
                    elif not (isinstance(g, int) and g == NG - 1):
                        split_w(g + 1, 0)
                    after(dve, squared, 4 * (h - 1))
                    take_vectors(h, j, vec_now_a)
                    after(dve, spilled[j], 32 * g)
                    after(dve, vec_now_a, h + 1)
                    for s in range(4):
                        w, half = divmod(s, 2)
                        after(dve, squared, 4 * h + s + 1)
                        nc.vector.tensor_scalar(qk_raw[:, j, w, half * HALF:(half + 1) * HALF], bank[4 * j + s][:, :],
                                                vec_now[:, j, w:w + 1], vec_now[:, j, 2 + w:3 + w],
                                                ALU.add, ALU.mult).then_inc(scaled, 1)

            loop_peeled(dve, NG, pair_a)

            def lo_v(n, s):
                after(dve, v_hi, n + 1)
                ps = first_v_bank[s] if isinstance(n, int) and n < NT else aux_bank[s % 2]
                nc.vector.tensor_tensor(v[1][:, s, :], ps[:, 0:2 * HD], v[0][:, s, :].bitcast(F32),
                                        ALU.subtract).then_inc(v_lo, 1)

            for s in range(2):
                lo_v(s, s)
            dve.wait_ge(rms_mm, 1)
            nc.vector.tensor_scalar(rms[:, 0, :], bank[2][:, 0:2 * NT], 1.0 / INNER, RMS_EPS, ALU.mult, ALU.add).then_inc(rms_var, 1)
            dve.wait_ge(rms_root, 1)
            link(nc.vector.reciprocal(rms[:, 2, :], rms[:, 1, :]))
            newton(rms[:, 2, :], rms[:, 0, :], rms[:, 3, :]).then_inc(rms_cols, 1)
            dve.wait_ge(rms_cols, 1)
            nc.vector.tensor_scalar(qscale[:, 0, :], rms[:, 2, 0:NT], SOFTMAX_SCALE, None, ALU.mult)
            nc.vector.tensor_scalar(qscale[:, 1, :], rms[:, 2, 0:NT], -SOFTMAX_SCALE, None, ALU.mult)
            lo_v(2, 2)
            dve.wait_ge(rk_mm, 1)
            nc.vector.tensor_copy(rk[:, 0:HALF], bank[0][:, :]).then_inc(rk_ready, 1)
            dve.wait_ge(qk_in[0], 32)
            dve.wait_ge(rk_ready, 2)
            nc.vector.tensor_tensor(qk_raw[:, 0, 1, :], qk_raw[:, 0, 1, :], rk[:, :], ALU.mult).then_inc(k_normed, 1)
            lo_v(3, 3)
            dve.wait_ge(qk_hi, 2)
            nc.vector.tensor_tensor(qks[1][:, 0, 1, :], qk_raw[:, 0, 1, :], qks[0][:, 0, 1, :].bitcast(F32),
                                    ALU.subtract).then_inc(qk_lo, 1)
            lo_v(4, 4)

            def maxima(u, i):
                b = i % B
                after(dve, score_mm, u + 1)
                nc.vector.tensor_reduce(rowmax[:, i % 2, :], s_bank[i % 2][:, :].rearrange("p (q s) -> p q s", q=QT),
                                        AX.X, ALU.max).then_inc(max_done, 1)
                after(dve, max_done, u + 1)
                nc.vector.tensor_tensor(negmax[:, i % 2, :], rowmax[:, i % 2, :], qscale[:, 1, QT * b:QT * (b + 1)],
                                        ALU.mult).then_inc(negmax_done, 1)

            def normalise(u, i):
                after(dve, exp_done, QT * (u + 1))
                nc.vector.reciprocal(rowinv[:, i % 2, :], rowsum[:, i % 2, :]).then_inc(inv_done, 1)
                after(dve, inv_done, u + 1)
                for q in range(QT):
                    last = nc.vector.tensor_scalar(prob[:, i % 2, q, :], prob[:, i % 2, q, :], rowinv[:, i % 2, q:q + 1],
                                                   None, ALU.mult)
                last.then_inc(prob_ready, 1)

            def lo_pT(u, i):
                after(dve, pT_hi, u + 1)
                nc.vector.tensor_tensor(pT[1][:, i % 2, :, :], pT_bank[i % 2][:, :].rearrange("p (k q) -> p k q", k=QT),
                                        pT[0][:, i % 2, :, :].bitcast(F32), ALU.subtract).then_inc(pT_lo, 1)

            def lo_o(u, i, h):
                j, b = divmod(i, B)
                after(dve, o_hi, u + 1)
                after(dve, vec_now_b, h + 1)
                nc.vector.scalar_tensor_tensor(out=oT[1][:, j, b * S:(b + 1) * S], in0=o_bank[i % 2][:, 0:S],
                                               scalar=vec_now[:, j, 4:5], in1=oT[0][:, j, b * S:(b + 1) * S].bitcast(F32),
                                               op0=ALU.add, op1=ALU.subtract).then_inc(o_lo, 1)

            def add_attn(g, t):
                after(dve, wo_mm, 8 * g + t + 1)
                nc.vector.tensor_tensor(attn[:, t, :], aux_bank[t % 2][:, :], attn[:, t, :], ALU.add).then_inc(attn_added, 1)

            def residual(b, before_stats=lambda: None):
                two = (2 * b, 2 * b + 1)
                for t in two:
                    dve.wait_ge(wo_mm, 8 * (NG - 1) + t + 1)
                    dve.wait_ge(x_under, t + 1)
                    nc.vector.tensor_tensor(x_sb[:, t, :], last_bank[t][:, :], gates[:, 0, b, :], ALU.mult).then_inc(last_gated, 1)
                if b == B - 1:
                    for t in two:
                        dve.wait_ge(last_gated, t + 1)
                        nc.vector.tensor_tensor(x_sb[:, t, :], x_sb[:, t, :], attn[:, t, :], ALU.add).then_inc(last_x_done, 1)
                before_stats()
                for t in two:
                    if b == B - 1:
                        dve.wait_ge(last_x_done, t - 5)
                    else:
                        dve.wait_ge(x_done, t + 1)
                    last = nc.vector.bn_stats(stats[:, t, :], x_sb[:, t, :])
                link(last)
                for t in two:
                    last = nc.vector.bn_aggr(mv[:, t, :], stats[:, t, :])
                link(last)
                nc.vector.tensor_scalar(norm[:, 0, 2 * b:2 * b + 2], mv[:, 2 * b:2 * b + 2, 1], LN_EPS, None, ALU.add).then_inc(var2, 1)

            def norm_factors(b):
                two = slice(2 * b, 2 * b + 2)
                dve.wait_ge(root2, b + 1)
                link(nc.vector.reciprocal(norm[:, 2, two], norm[:, 1, two]))
                link(newton(norm[:, 2, two], norm[:, 0, two], norm[:, 3, two]))
                nc.vector.scalar_tensor_tensor(out=norm[:, 3, two], in0=mv[:, two, 0], scalar=-1.0, in1=norm[:, 2, two],
                                               op0=ALU.mult, op1=ALU.mult).then_inc(norm2_ready, 1)

            maxima(0, 0)
            lo_v(5, 5)
            maxima(1, 1)
            normalise(0, 0)
            normalise(1, 1)
            lo_v(6, 6)
            lo_pT(0, 0)
            maxima(2, 2)
            normalise(2, 2)

            def pair_b(g):
                first, last = isinstance(g, int) and g == 0, isinstance(g, int) and g == NG - 1
                for i in range(UNITS):
                    u = UNITS * g + i
                    if not (last and i + 1 >= UNITS):
                        lo_pT(u + 1, (i + 1) % UNITS)
                    if not (last and i + 3 >= UNITS):
                        maxima(u + 3, (i + 3) % UNITS)
                    if first and i == 0:
                        lo_v(7, 7)
                    if i < B and not first:
                        for t in (2 * i, 2 * i + 1):
                            add_attn(g - 1, t)
                    if not (last and i + 3 >= UNITS):
                        normalise(u + 3, (i + 3) % UNITS)
                    if i % B == 0:
                        after(dve, o_hi, UNITS * (g - 1) + i + B)
                        take_vectors(2 * g + i // B, i // B, vec_now_b)
                    if last:
                        for n in LAST_PAIR_BEFORE.get(i, ()):
                            lo_ffn(n)
                    lo_o(u, i, 2 * g + i // B)
                    if i >= B and not last:
                        for s in (2 * (i - B), 2 * (i - B) + 1):
                            lo_v(8 * (g + 1) + s, s)
                    if first and i == B - 1:
                        modulation(mod2, aux_bank[0], 1)
                        dve.wait_ge(bo_in, 16)
                    if first and i == UNITS - 1:
                        clamp_gates()
                    if last:
                        for n in LAST_PAIR_AFTER.get(i, ()):
                            lo_ffn(n)
                        if i > B:
                            residual(i - B - 1, before_stats=lambda: norm_factors(i - B - 2) if i > B + 1 else None)

            def lo_ffn(n):
                ps = aux_bank[n % 2]
                dve.wait_ge(ffn_hi, n + 1)
                if n == 0:
                    nc.vector.scalar_tensor_tensor(out=bT[1], in0=ps[:, :], scalar=lora_coef[:, 1:2], in1=bT[0].bitcast(F32),
                                                   op0=ALU.mult, op1=ALU.subtract).then_inc(ffn_lo, 1)
                else:
                    nc.vector.tensor_tensor(ffnT[1][:, n - 1, :], ps[:, :], ffnT[0][:, n - 1, :].bitcast(F32),
                                            ALU.subtract).then_inc(ffn_lo, 1)

            def clamp_gates():
                for m in range(2):
                    ps = aux_bank[m][0:B, :]
                    dve.wait_ge(gate_mm, m + 1)
                    link(nc.vector.tensor_scalar(gate_sign[:, m, :], ps, 0.0, 2.0, ALU.is_ge, ALU.mult))
                    link(nc.vector.tensor_scalar(gate_sign[:, m, :], gate_sign[:, m, :], 1.0, None, ALU.subtract))
                    link(nc.vector.tensor_tensor(gate_row[:, m, :], ps, gate_sign[:, m, :], ALU.mult))
                    nc.vector.scalar_tensor_tensor(out=gate_row[:, m, :], in0=gate_row[:, m, :], scalar=0.25,
                                                   in1=gate_sign[:, m, :], op0=ALU.max, op1=ALU.mult).then_inc(gate_ready, 1)

            loop_peeled(dve, NG, pair_b)

            def lo_h2(b):
                for half in range(2):
                    n = 2 * b + half
                    dve.wait_ge(h2_hi, n + 1)
                    part = (slice(None), slice(2 * half, 2 * half + 2), slice(b * S, (b + 1) * S))
                    nc.vector.tensor_tensor(hT[1][part], h2_tmp[:, n % 2, :].rearrange("p (k t) -> p k t", k=2),
                                            hT[0][part].bitcast(F32), ALU.subtract).then_inc(h2_lo, 1)

            def finish(b):
                for t in (2 * b, 2 * b + 1):
                    dve.wait_ge(out_mm, t + 1)
                    nc.vector.tensor_tensor(attn[:, t, :], bank[4 + t % 2][:, :], gates[:, 1, b, :], ALU.mult).then_inc(out_gated, 1)
                    if t >= 6:
                        dve.wait_ge(out_gated, t + 1)
                        dve.wait_ge(x_biased, t + 1)
                        nc.vector.tensor_tensor(attn[:, t, :], attn[:, t, :], x_sb[:, t, :], ALU.add).then_inc(out_ready_last, 1)

            lo_h2(0)
            norm_factors(2)
            residual(3)
            lo_h2(1)
            norm_factors(3)
            finish(0)
            lo_h2(2)
            finish(1)
            lo_h2(3)
            finish(2)
            finish(3)

        @block.tensor
        def _(pe):
            mm = nc.tensor.matmul

            def product(out_, lhs, rhs, steps, between=lambda i: None):
                n = len(steps) * len(PARTS)
                for i, (k, (a, b)) in enumerate([(k, p) for k in steps for p in PARTS]):
                    between(i)
                    last = mm(out_, lhs(a, k), rhs(b, k), start=i == 0, stop=i == n - 1)
                return last

            pe.wait_ge(ident_ready, 2)
            pe.wait_ge(c_in, 16)
            for k in range(KT):
                last = nc.tensor.transpose(bank[0][:, k * B:(k + 1) * B], c_row[:, k * P:(k + 1) * P], ident[0:B, 0:B])
            last.then_inc(cT_mm, 1)

            def mod_rows(ps, w, m, tiles=range(KT)):
                for k in tiles:
                    last = mm(ps[0:B, :], cT[:, k, :], w[:, k, m * D:(m + 1) * D], start=k == 0, stop=k == KT - 1)
                return last

            def mod_columns(ps):
                for m in range(2):
                    for k in range(KT):
                        n = m * KT + k
                        last = nc.tensor.transpose(ps[:, n * B:(n + 1) * B], mod_row[:, m, k * P:(k + 1) * P], ident[0:B, 0:B])
                return last

            def x_transposes(n):
                half, k = divmod(n, KT)
                pe.wait_ge(xn_ready, 4 * half + 4)
                after(pe, h_affine, 2 * (n - KT) + 2)
                for t in range(4):
                    last = nc.tensor.transpose(bank[X_BANK[n]][:, t * P:(t + 1) * P], x_sb[:, 4 * half + t, k * P:(k + 1) * P], ident[:])
                last.then_inc(hT_mm, 1)

            pe.wait_ge(cT_ready, 1)
            for k in range(KT):
                if k == KT // 2:
                    for n in range(KT):
                        x_transposes(n)
                pe.wait_ge(mod1_in[k], 16)
                for m in range(2):
                    last = mod_rows(bank[4 + 2 * m], wmod_a, m, (k,))
            last.then_inc(mod_row_mm, 1)
            pe.wait_ge(small_in, 96)
            for i in range(5):
                last = nc.tensor.transpose(bank[2][:, i * H:(i + 1) * H], vec_rows[:, i, :], ident[0:H, 0:H])
            last.then_inc(vec_mm, 1)
            pe.wait_ge(mod_row_ready, 2)
            pe.wait_ge(vec_ready, 1)
            mod_columns(bank[2][:, 5 * H:]).then_inc(mod_mm, 1)
            pe.wait_ge(mod_ready, 2)

            def project_qk(j, w, k, i, half):
                a, b = PARTS[i]
                first, done = k == 0 and i == 0, k == KT - 1 and i == len(PARTS) - 1
                ins = mm(bank[4 * j + 2 * w + half][:, :], ws[a][:, j, w, k, :],
                         hT[b][:, k, half * HALF:(half + 1) * HALF], start=first, stop=done)
                if done:
                    ins.then_inc(proj_mm, 1)

            def first_pair():
                for half in range(2):
                    for j in range(2):
                        for k in range(KT):
                            if (half, j, k) == (0, 1, KT - 1):
                                for n in range(KT, 2 * KT):
                                    x_transposes(n)
                            for w in range(2):
                                if half == 0 and k == 0:
                                    pe.wait_ge(w_lo, 2 * j + w + 1)
                                if j == 0:
                                    pe.wait_ge(hT_lo_ready, KT * half + max(k + 1, half * (w + 1)))
                                for i in range(len(PARTS)):
                                    project_qk(j, w, k, i, half)

            def pair_a(g):
                if isinstance(g, int) and g == 0:
                    first_pair()
                    return
                for j in range(2):
                    h = 2 * g + j
                    for w in range(2):
                        after(pe, w_lo, 2 * h + w + 1)
                        after(pe, scaled, 4 * (h - 2) + 2 * w + 2)
                        for k in range(KT):
                            for i in range(len(PARTS)):
                                for half in range(2):
                                    project_qk(j, w, k, i, half)

            loop_peeled(pe, NG, pair_a)

            def values(g, s, between=lambda i: None):
                n = 8 * g + s
                after(pe, wv_lo, g + 1)
                if s == 0 and isinstance(g, int) and g == 1:
                    pe.wait_ge(mod_ready, 4)
                if isinstance(g, int) and g == 0:
                    if s < 4:
                        pe.wait_ge(scaled, 4 * (H - 1 + s // 2))
                    else:
                        pe.wait_ge(v_lo, s - 1)
                elif s >= 2 or (isinstance(g, int) and g == 1):
                    after(pe, v_lo, n - 1)
                else:
                    after(pe, attn_added, 8 * (g - 2) + 6 + s + 1)
                ps = first_v_bank[s] if isinstance(g, int) and g == 0 else aux_bank[s % 2]
                product(ps[:, 0:2 * HD], lambda a, k: hT[a][:, k, s * P:(s + 1) * P],
                        lambda b, k: wvs[b][:, k, :], range(KT), between).then_inc(v_mm, 1)

            values(0, 0)
            def sum_columns(w):
                def between(i):
                    t = w * NT + i - 2
                    if not w * NT <= t < (w + 1) * NT:
                        return
                    if t % 4 == 0:
                        pe.wait_ge(summed, 4 * (H - 1) + t // 4 + 1)
                    last = mm(bank[2][:, t:t + 1], sumsq[:, t // 4, (t % 4) * P:(t % 4 + 1) * P], ones[:, 0:1], start=True, stop=True)
                    if t == 2 * NT - 1:
                        last.then_inc(rms_mm, 1)
                return between

            values(0, 1, sum_columns(0))
            values(0, 2, sum_columns(1))
            values(0, 3)
            pe.wait_ge(rms_cols, 1)
            for t in range(NT):
                last = mm(bank[t // 4][:, (t % 4) * P:(t % 4 + 1) * P], rms[:, 2, NT + t:NT + t + 1].to_broadcast([P, P]),
                          ident[:], start=True, stop=True)
            last.then_inc(rk_mm, 1)
            for s in range(4, 6):
                values(0, s)

            def scores(g, u, i):
                j, b = divmod(i, B)
                if b == 0:
                    after(pe, qk_lo, 2 * (2 * g + j) + 2)
                for q in range(QT):
                    rows = slice(b * S + q * P, b * S + (q + 1) * P)
                    last = product(s_bank[i % 2][:, q * S:(q + 1) * S], lambda a, _: qks[a][:, j, 0, rows],
                                   lambda a, _: qks[a][:, j, 1, b * S:(b + 1) * S], [0])
                last.then_inc(score_mm, 1)

            def transposes(u, i):
                after(pe, prob_ready, u + 1)
                after(pe, pT_lo, u - 1)
                for k in range(QT):
                    for q in range(QT):
                        last = nc.tensor.transpose(pT_bank[i % 2][:, k * S + q * P:k * S + (q + 1) * P],
                                                   prob[:, i % 2, q, k * P:(k + 1) * P], ident[:])
                last.then_inc(pT_mm, 1)

            def weigh(g, u, i):
                j, b = divmod(i, B)
                after(pe, pT_lo, u + 1)
                after(pe, v_lo, 8 * g + 2 * b + 2)
                after(pe, o_lo, u - 1)
                product(o_bank[i % 2][:, 0:S], lambda a, k: v[a][:, 2 * b + k, j * HD:(j + 1) * HD],
                        lambda a, k: pT[a][:, i % 2, k, :], range(QT)).then_inc(o_mm, 1)

            def project(g, t):
                after(pe, wo_lo, g + 1)
                after(pe, o_lo, 8 * g + B + t // 2 + 1)
                if isinstance(g, int) and g == NG - 1:
                    if t < 2:
                        pe.wait_ge(ffn_lo, 5)
                    elif t < 4:
                        pe.wait_ge(last_gated, t - 1)
                    elif t < 6:
                        pe.wait_ge(pT_lo, NU)
                    else:
                        pe.wait_ge(last_gated, t - 3)
                elif t >= 2:
                    after(pe, attn_added, 8 * g + t - 1)
                else:
                    after(pe, v_lo, 8 * (g + 1) + 6 + t + 1)
                    pe.wait_ge(gate_ready, t + 1)
                ps = last_bank[t] if isinstance(g, int) and g == NG - 1 else aux_bank[t % 2]
                product(ps[:, :], lambda a, j: oT[a][:, j, t * P:(t + 1) * P],
                        lambda a, j: wos[a][:, j, :], range(2)).then_inc(wo_mm, 1)

            def ffn_weights(n):
                ps = aux_bank[n % 2]
                if n < 2:
                    pe.wait_ge(attn_added, 8 * (NG - 2) + 6 + n + 1)
                else:
                    pe.wait_ge(ffn_lo, n - 1)
                if n == 0:
                    pe.wait_ge(lora_in, 16 * (1 + NR))
                    for i in range(KT):
                        last = nc.tensor.transpose(ps[:, i * P:(i + 1) * P], lora_b_raw[:, i * P:(i + 1) * P], ident[:])
                else:
                    cols = slice((n - 1) * P, n * P)
                    pe.wait_ge(ffn_lo, 1)
                    pe.wait_ge(lora_lo, 1)
                    for i, (a, b) in enumerate(PARTS):
                        mm(ps[:, :], lora_as[a][:, cols], bT[b], start=i == 0, stop=False)
                    pe.wait_ge(ffn_in, 32)
                    for i in range(KT):
                        last = mm(ps[:, i * P:(i + 1) * P], ffn_raw[i // 2][:, i % 2, cols], ident[:], start=False, stop=i == KT - 1)
                last.then_inc(ffn_mm, 1)

            def gate_rows():
                pe.wait_ge(gate_w_in, 32)
                for m in range(2):
                    pe.wait_ge(v_lo, 16 + m - 1)
                    mod_rows(aux_bank[m], wmod_b, m).then_inc(gate_mm, 1)

            pe.wait_ge(rk_ready, 2)
            scores(0, 0, 0)
            scores(0, 1, 1)
            values(0, 6)
            transposes(0, 0)
            scores(0, 2, 2)

            def pair_b(g):
                first, last = isinstance(g, int) and g == 0, isinstance(g, int) and g == NG - 1
                for i in range(UNITS):
                    u = UNITS * g + i
                    if not (last and i + 1 >= UNITS):
                        transposes(u + 1, (i + 1) % UNITS)
                    if not (last and i + 3 >= UNITS):
                        scores(g + (i + 3) // UNITS, u + 3, (i + 3) % UNITS)
                    if i < B and not first:
                        for t in (2 * i, 2 * i + 1):
                            project(g - 1, t)
                    if last:
                        for n in LAST_PAIR_BEFORE.get(i, ()):
                            ffn_weights(n)
                    if i < B and first:
                        if i == 0:
                            values(0, 7)
                        elif i < 3:
                            pe.wait_ge(mod2_in, 16)
                            pe.wait_ge(v_lo, 8)
                            mod_rows(aux_bank[i - 1], wmod_b, i - 1).then_inc(mod_row_mm, 1)
                        else:
                            pe.wait_ge(mod_row_ready, 4)
                            mod_columns(aux_bank[0]).then_inc(mod_mm, 1)
                    weigh(g, u, i)
                    if last:
                        for n in LAST_PAIR_AFTER.get(i, ()):
                            ffn_weights(n)
                    if i >= B and not last:
                        for s in (2 * (i - B), 2 * (i - B) + 1):
                            values(g + 1, s)
                    if first and i == UNITS - 1:
                        gate_rows()
                    if i > B and last:
                        for t in (2 * (i - B - 1), 2 * (i - B - 1) + 1):
                            project(g, t)

            loop_peeled(pe, NG, pair_b)

            def h2_transposes(b):
                pe.wait_ge(xn2, 2 * b + 2)
                for half in range(2):
                    n = 2 * b + half
                    after(pe, h2_affine, 2 * (n - 2) + 2)
                    for i in range(2):
                        for q in range(QT):
                            k = 2 * half + i
                            last = nc.tensor.transpose(bank[half][:, i * S + q * P:i * S + (q + 1) * P],
                                                       attn[:, 2 * b + q, k * P:(k + 1) * P], ident[:])
                    last.then_inc(h2_mm, 1)

            def ffn(b):
                for t in (2 * b, 2 * b + 1):
                    ps = bank[4 + t % 2]
                    after(pe, out_gated, t - 1)
                    pe.wait_ge(h2_lo, 2 * b + 2)
                    product(ps[:, :], lambda a, k: hT[a][:, k, t * P:(t + 1) * P], lambda a, k: ffnT[a][:, k, :],
                            range(KT)).then_inc(out_mm, 1)

            h2_transposes(0)
            for t in range(NT - 2, NT):
                project(NG - 1, t)
            for b in range(B):
                if b + 1 < B:
                    h2_transposes(b + 1)
                ffn(b)


_INS = ["L0_attn_hidden_states", "L0_attn_Wq", "L0_attn_bq", "L0_attn_Wk", "L0_attn_bk", "L0_attn_Wv", "L0_attn_bv",
        "L0_attn_Wo", "L0_attn_bo", "L0_attn_gq", "L0_attn_gk", "L0_ffn_lora_A", "L0_ffn_lora_B", "L0_ffn_W",
        "L0_ffn_bias", "L0_ffn_lora_weights", "L0_c", "L0_wmod"]


def kernel(**inputs):
    import numpy as np
    import concourse.bacc as bacc
    from concourse.bass_utils import run_bass_kernel_spmd

    nc = bacc.Bacc("TRN2", target_bir_lowering=False, num_devices=1)
    arrays, args = {}, []
    for name in _INS:
        a = np.ascontiguousarray(inputs[name])
        arrays[f"in_{name}"] = a
        args.append(nc.dram_tensor(f"in_{name}", a.shape, mybir.dt.from_np(a.dtype), kind="ExternalInput").ap())
    args.append(nc.dram_tensor("out_x", (B, S, D), F32, kind="ExternalOutput").ap())
    adaln_block(nc, *args)
    r = run_bass_kernel_spmd(nc, [arrays], core_ids=[0])
    return r.results[0]["out_x"]
```
